# Optimizing a Trainium2 kernel written in Bass

```python
import numpy as np
import jax
import jax.numpy as jnp

def _softmax(x, axis=-1):
    return jax.nn.softmax(x, axis=axis)

def _gelu(x):
    return jax.nn.gelu(x, approximate=True)

def _silu(x):
    return jax.nn.silu(x)

def _sigmoid(x):
    return jax.nn.sigmoid(x)

def _layernorm(x, axis=-1, eps=1e-05):
    m = jnp.mean(x, axis=axis, keepdims=True)
    v = jnp.var(x, axis=axis, keepdims=True)
    return (x - m) / jnp.sqrt(v + eps)

def _scatter_add(tgt, idx, src, axis=0):
    return tgt.at[idx].add(src)

def _segment_sum(src, seg, n):
    return jax.ops.segment_sum(src, seg, n)
kernel_name = 'mk_macaron_d1_jaxref_r8_a60bdd'

def setup_inputs(seed: int=0):
    np.random.seed(seed)
    _w = jnp.asarray

    def _L0_attn_setup():
        import jax, jax.numpy as jnp
        import numpy as np
        N_HEAD = 16
        PAGE_SIZE = 32
        ROPE_THETA = 10000.0

        def _rope_tables(T, D, dtype):
            inv = 1.0 / ROPE_THETA ** (np.arange(0, D, 2, dtype=np.float32) / D)
            ang = np.outer(np.arange(T, dtype=np.float32), inv)
            return (jnp.asarray(np.cos(ang), dtype), jnp.asarray(np.sin(ang), dtype))

        def _apply_rope(x, cos, sin):
            x1 = x[..., 0::2]
            x2 = x[..., 1::2]
            c = cos[None, :, None, :]
            s = sin[None, :, None, :]
            out = jnp.stack([x1 * c - x2 * s, x1 * s + x2 * c], axis=-1)
            return out.reshape(x.shape)
        key = jax.random.key(seed)
        ks = jax.random.split(key, 6)
        B, T, E = (2, 256, 128)
        L = E // 2
        sc = lambda fan: 1.0 / np.sqrt(fan)
        return {'x': jax.random.normal(ks[0], (B, T, E), jnp.float32), 'wq': jax.random.normal(ks[1], (E, E), jnp.float32) * sc(E), 'w_down': jax.random.normal(ks[2], (E, L), jnp.float32) * sc(E), 'wk_up': jax.random.normal(ks[3], (L, E), jnp.float32) * sc(L), 'wv_up': jax.random.normal(ks[4], (L, E), jnp.float32) * sc(L), 'wo': jax.random.normal(ks[5], (E, E), jnp.float32) * sc(E)}
    _L0_attn_in = _L0_attn_setup()

    def _L0_ffn_setup():
        import jax, jax.numpy as jnp
        import numpy as np
        D = 128
        H = 4
        HD = D // H
        E = 8
        FF = 512
        CAP_FACTOR = 1.0

        def _ln(x, g, b, eps=1e-05):
            mu = jnp.mean(x, -1, keepdims=True)
            v = jnp.mean((x - mu) ** 2, -1, keepdims=True)
            return (x - mu) * jax.lax.rsqrt(v + eps) * g + b

        def _mha(x, w, b, ow, ob):
            L, N, _ = x.shape
            qkv = x @ w.T + b
            q, k, v = jnp.split(qkv, 3, axis=-1)
            rh = lambda t: t.reshape(L, N, H, HD).transpose(1, 2, 0, 3)
            q, k, v = (rh(q), rh(k), rh(v))
            scores = jnp.einsum('nhld,nhmd->nhlm', q, k) / np.float32(np.sqrt(HD))
            attn = jax.nn.softmax(scores, axis=-1)
            o = jnp.einsum('nhlm,nhmd->nhld', attn, v).transpose(2, 0, 1, 3).reshape(L, N, D)
            return o @ ow.T + ob

        def _moe(x, wg, w1, b1, w2, b2):
            L, N, _ = x.shape
            S = L * N
            cap = int(CAP_FACTOR * S) // E
            xf = x.reshape(S, D)
            gates = jax.nn.softmax(xf @ wg, axis=-1)
            idx = jnp.argmax(gates, axis=-1)
            mask1 = jax.nn.one_hot(idx, E, dtype=x.dtype)
            loc = jnp.sum((jnp.cumsum(mask1, 0) - 1.0) * mask1, -1).astype(jnp.int32)
            keep = loc < cap
            gate_val = jnp.take_along_axis(gates, idx[:, None], -1)[:, 0]
            slot = jnp.where(keep, idx.astype(jnp.int32) * cap + loc, E * cap)
            disp = jnp.zeros((E * cap, D), x.dtype).at[slot].set(xf, mode='drop')
            disp = disp.reshape(E, cap, D)
            h = jnp.einsum('ecd,edf->ecf', disp, w1) + b1[:, None, :]
            y = (jnp.einsum('ecf,efd->ecd', h, w2) + b2[:, None, :]).reshape(E * cap, D)
            out = jnp.where(keep[:, None], gate_val[:, None] * y[jnp.minimum(slot, E * cap - 1)], 0.0)
            return out.reshape(L, N, D)
        key = jax.random.key(seed)
        ks = jax.random.split(key, 8)
        L, N = (128, 16)
        s = 0.02
        return {'x': jax.random.normal(ks[0], (L, N, D), jnp.float32), 'in_proj_w': jax.random.normal(ks[1], (3 * D, D), jnp.float32) * s, 'in_proj_b': jnp.zeros((3 * D,), jnp.float32), 'out_proj_w': jax.random.normal(ks[2], (D, D), jnp.float32) * s, 'out_proj_b': jnp.zeros((D,), jnp.float32), 'ln1_g': jnp.ones((D,), jnp.float32), 'ln1_b': jnp.zeros((D,), jnp.float32), 'ln2_g': jnp.ones((D,), jnp.float32), 'ln2_b': jnp.zeros((D,), jnp.float32), 'wg': jax.random.normal(ks[3], (D, E), jnp.float32) * s, 'w1': jax.random.normal(ks[4], (E, D, FF), jnp.float32) * s, 'b1': jnp.zeros((E, FF), jnp.float32), 'w2': jax.random.normal(ks[5], (E, FF, D), jnp.float32) * s, 'b2': jnp.zeros((E, D), jnp.float32)}
    _L0_ffn_in = _L0_ffn_setup()
    _d = {'L0_attn_x': _L0_attn_in['x'], 'L0_attn_wq': _L0_attn_in['wq'], 'L0_attn_w_down': _L0_attn_in['w_down'], 'L0_attn_wk_up': _L0_attn_in['wk_up'], 'L0_attn_wv_up': _L0_attn_in['wv_up'], 'L0_attn_wo': _L0_attn_in['wo'], 'L0_ffn_in_proj_w': _L0_ffn_in['in_proj_w'], 'L0_ffn_in_proj_b': _L0_ffn_in['in_proj_b'], 'L0_ffn_out_proj_w': _L0_ffn_in['out_proj_w'], 'L0_ffn_out_proj_b': _L0_ffn_in['out_proj_b'], 'L0_ffn_ln1_g': _L0_ffn_in['ln1_g'], 'L0_ffn_ln1_b': _L0_ffn_in['ln1_b'], 'L0_ffn_ln2_g': _L0_ffn_in['ln2_g'], 'L0_ffn_ln2_b': _L0_ffn_in['ln2_b'], 'L0_ffn_wg': _L0_ffn_in['wg'], 'L0_ffn_w1': _L0_ffn_in['w1'], 'L0_ffn_b1': _L0_ffn_in['b1'], 'L0_ffn_w2': _L0_ffn_in['w2'], 'L0_ffn_b2': _L0_ffn_in['b2']}
    _x0 = _d['L0_attn_x']
    _d['L0_attn_x'] = jax.random.normal(jax.random.fold_in(jax.random.key(seed), 1), (1, 2048, 128), dtype=_x0.dtype)
    del _x0
    return _d

def reference(L0_attn_x, L0_attn_wq, L0_attn_w_down, L0_attn_wk_up, L0_attn_wv_up, L0_attn_wo, L0_ffn_in_proj_w, L0_ffn_in_proj_b, L0_ffn_out_proj_w, L0_ffn_out_proj_b, L0_ffn_ln1_g, L0_ffn_ln1_b, L0_ffn_ln2_g, L0_ffn_ln2_b, L0_ffn_wg, L0_ffn_w1, L0_ffn_b1, L0_ffn_w2, L0_ffn_b2):

    def _L0_attn_ref(x, wq, w_down, wk_up, wv_up, wo):
        import jax, jax.numpy as jnp
        import numpy as np
        N_HEAD = 16
        PAGE_SIZE = 32
        ROPE_THETA = 10000.0

        def _rope_tables(T, D, dtype):
            inv = 1.0 / ROPE_THETA ** (np.arange(0, D, 2, dtype=np.float32) / D)
            ang = np.outer(np.arange(T, dtype=np.float32), inv)
            return (jnp.asarray(np.cos(ang), dtype), jnp.asarray(np.sin(ang), dtype))

        def _apply_rope(x, cos, sin):
            x1 = x[..., 0::2]
            x2 = x[..., 1::2]
            c = cos[None, :, None, :]
            s = sin[None, :, None, :]
            out = jnp.stack([x1 * c - x2 * s, x1 * s + x2 * c], axis=-1)
            return out.reshape(x.shape)
        B, T, E = x.shape
        H = N_HEAD
        D = E // H
        q = (x @ wq).reshape(B, T, H, D)
        lat = x @ w_down
        k = (lat @ wk_up).reshape(B, T, H, D)
        v = (lat @ wv_up).reshape(B, T, H, D)
        cos, sin = _rope_tables(T, D, x.dtype)
        q = _apply_rope(q, cos, sin)
        k = _apply_rope(k, cos, sin)
        scale = 1.0 / jnp.sqrt(jnp.asarray(D, x.dtype))
        scores = jnp.einsum('bqhd,bkhd->bhqk', q, k) * scale
        pages = jnp.arange(T) // PAGE_SIZE
        allowed = pages[None, :] <= pages[:, None]
        scores = jnp.where(allowed[None, None], scores, jnp.finfo(scores.dtype).min)
        attn = jax.nn.softmax(scores, axis=-1)
        out = jnp.einsum('bhqk,bkhd->bqhd', attn, v).reshape(B, T, E)
        return out @ wo

    def _L0_ffn_ref(x, in_proj_w, in_proj_b, out_proj_w, out_proj_b, ln1_g, ln1_b, ln2_g, ln2_b, wg, w1, b1, w2, b2):
        import jax, jax.numpy as jnp
        import numpy as np
        D = 128
        H = 4
        HD = D // H
        E = 8
        FF = 512
        CAP_FACTOR = 1.0

        def _ln(x, g, b, eps=1e-05):
            mu = jnp.mean(x, -1, keepdims=True)
            v = jnp.mean((x - mu) ** 2, -1, keepdims=True)
            return (x - mu) * jax.lax.rsqrt(v + eps) * g + b

        def _mha(x, w, b, ow, ob):
            L, N, _ = x.shape
            qkv = x @ w.T + b
            q, k, v = jnp.split(qkv, 3, axis=-1)
            rh = lambda t: t.reshape(L, N, H, HD).transpose(1, 2, 0, 3)
            q, k, v = (rh(q), rh(k), rh(v))
            scores = jnp.einsum('nhld,nhmd->nhlm', q, k) / np.float32(np.sqrt(HD))
            attn = jax.nn.softmax(scores, axis=-1)
            o = jnp.einsum('nhlm,nhmd->nhld', attn, v).transpose(2, 0, 1, 3).reshape(L, N, D)
            return o @ ow.T + ob

        def _moe(x, wg, w1, b1, w2, b2):
            L, N, _ = x.shape
            S = L * N
            cap = int(CAP_FACTOR * S) // E
            xf = x.reshape(S, D)
            gates = jax.nn.softmax(xf @ wg, axis=-1)
            idx = jnp.argmax(gates, axis=-1)
            mask1 = jax.nn.one_hot(idx, E, dtype=x.dtype)
            loc = jnp.sum((jnp.cumsum(mask1, 0) - 1.0) * mask1, -1).astype(jnp.int32)
            keep = loc < cap
            gate_val = jnp.take_along_axis(gates, idx[:, None], -1)[:, 0]
            slot = jnp.where(keep, idx.astype(jnp.int32) * cap + loc, E * cap)
            disp = jnp.zeros((E * cap, D), x.dtype).at[slot].set(xf, mode='drop')
            disp = disp.reshape(E, cap, D)
            h = jnp.einsum('ecd,edf->ecf', disp, w1) + b1[:, None, :]
            y = (jnp.einsum('ecf,efd->ecd', h, w2) + b2[:, None, :]).reshape(E * cap, D)
            out = jnp.where(keep[:, None], gate_val[:, None] * y[jnp.minimum(slot, E * cap - 1)], 0.0)
            return out.reshape(L, N, D)
        y1 = _ln(x + _mha(x, in_proj_w, in_proj_b, out_proj_w, out_proj_b), ln1_g, ln1_b)
        y2 = _ln(y1 + _moe(y1, wg, w1, b1, w2, b2), ln2_g, ln2_b)
        return y2
    x = L0_attn_x
    x = x + 0.5 * _L0_ffn_ref(_layernorm(x, axis=-1), L0_ffn_in_proj_w, L0_ffn_in_proj_b, L0_ffn_out_proj_w, L0_ffn_out_proj_b, L0_ffn_ln1_g, L0_ffn_ln1_b, L0_ffn_ln2_g, L0_ffn_ln2_b, L0_ffn_wg, L0_ffn_w1, L0_ffn_b1, L0_ffn_w2, L0_ffn_b2)
    x = x + _L0_attn_ref(_layernorm(x, axis=-1), L0_attn_wq, L0_attn_w_down, L0_attn_wk_up, L0_attn_wv_up, L0_attn_wo)
    x = x + 0.5 * _L0_ffn_ref(_layernorm(x, axis=-1), L0_ffn_in_proj_w, L0_ffn_in_proj_b, L0_ffn_out_proj_w, L0_ffn_out_proj_b, L0_ffn_ln1_g, L0_ffn_ln1_b, L0_ffn_ln2_g, L0_ffn_ln2_b, L0_ffn_wg, L0_ffn_w1, L0_ffn_b1, L0_ffn_w2, L0_ffn_b2)
    return x

_drawn_inputs = setup_inputs


def setup_inputs(seed=0):
    import zlib

    import numpy as np

    out = dict(_drawn_inputs(seed))
    spreads = {'L0_ffn_in_proj_b': (0.0, 0.493),
     'L0_ffn_out_proj_b': (0.0, 0.1),
     'L0_ffn_ln1_g': (1.0, 0.2),
     'L0_ffn_ln1_b': (0.0, 0.1),
     'L0_ffn_ln2_g': (1.0, 0.2),
     'L0_ffn_ln2_b': (0.0, 0.1),
     'L0_ffn_b1': (0.0, 0.8),
     'L0_ffn_b2': (0.0, 0.8)}
    factors = {'L0_ffn_wg': 4.474, 'L0_ffn_w1': 5.661, 'L0_ffn_w2': 5.181}
    for name, (base, spread) in spreads.items():
        noise = np.random.default_rng([zlib.crc32(name.encode()), seed]).standard_normal(out[name].shape)
        drawn = base * np.exp(spread * noise) if base else spread * noise
        out[name] = jnp.asarray(drawn.astype(out[name].dtype))
    for name, factor in factors.items():
        out[name] = (out[name] * factor).astype(out[name].dtype)
    return out
```

```python
from contextlib import ExitStack

import numpy as np
import concourse.bass as bass
from concourse import mybir
from concourse.alu_op_type import AluOpType as ALU

ACT = mybir.ActivationFunctionType
AX = mybir.AxisListType.X
F32 = mybir.dt.float32
BF16 = mybir.dt.bfloat16
I32 = mybir.dt.int32

P = 128
D = 128
S = 2048
T = S // P
G = 4
GT = T // G
GW = GT * P
E = 8
FF = 512
FC = FF // P
CAP = S // E
H = 16
HD = D // H
NG = 4
GH = H // NG
PAGE = 32
PAGES = S // PAGE
EPS = 1e-5
SCALE = float(HD) ** -0.5
SAFE = 40.0
MASKED = -1e30
Q_PIECE = (0, 0, 0, 1, 1, 2)
K_PIECE = (0, 1, 2, 0, 1, 0)
SHIFT_ROW = len(Q_PIECE) * HD
MASK_ROW = P - PAGES
VC = 32


def score_banks():
    banks = []
    for c in range(G):
        for j in range(GT * c):
            banks += [[(h, j, GW * c, GW, 0)] for h in range(GH)]
        j, q = GT * c, GW * c
        banks += [[(h, j, q, 4 * P, 0)] for h in range(GH)]
        banks += [[(h, j + 1, q + P, 3 * P, 0), (h, j + 3, q + 3 * P, P, 3 * P)] for h in range(GH)]
        banks += [[(h, j + 2, q + 2 * P, 2 * P, 0), (h + 1, j + 2, q + 2 * P, 2 * P, 2 * P)]
                  for h in range(0, GH, 2)]
    return banks


BANKS = score_banks()
SETS = 2
NE = SETS * len(BANKS) // 2
NB = SETS * len(BANKS) // 4
EB = 3
PB = 4
OB = 2
LAG = 2
assert len(BANKS) % 4 == 0 and NB % PB == 0


def chunk_of(block):
    return block[2] // GW


def previous_exp(n):
    return n - EB if n >= EB else max(m for m in range(NE) if m % EB == n % EB) - NE


def build(nc, a, out):
    with ExitStack() as ctx:
        def sb(name, shape, dt=F32):
            return ctx.enter_context(nc.sbuf_tensor(name, shape, dt))

        def sem(name):
            return ctx.enter_context(nc.semaphore(name))

        ps = ctx.enter_context(nc.psum_tensor("ps", [P, 8, 512], F32))

        ident = sb("ident", [P, P])
        tri_bf = sb("tri_bf", [P, 2, P], BF16)
        tile_is = sb("tile_is", [P, T])
        rank = sb("rank", [P, T, E])
        neg_half = sb("neg_half", [P, GT])
        w_mha = sb("w_mha", [P, D])
        b_mha = sb("b_mha", [P, D])
        g1c = sb("g1c", [P, 2])
        lnb = sb("lnb", [P, 4, D])
        wg = sb("wg", [P, E])
        w12 = sb("w12", [P, E * D])
        b12 = sb("b12", [P, D])
        b12_big = sb("b12_big", [P, T, D])
        wqo = sb("wqo", [P, 2, D])
        wdu = sb("wdu", [64, 3, D])
        wkv = sb("wkv", [P, 2, D])
        wsw = sb("wsw", [P, 2, D])
        x_tm = sb("x_tm", [P, T, D])
        trio = sb("trio", [P, 3 * S])
        xT = trio[:, 0:S]
        sin = trio[:, S:2 * S]
        cos = trio[:, 2 * S:3 * S]
        attn_tm = trio[:, 2 * S:3 * S].rearrange("p (t d) -> p t d", d=D)
        stats = sb("stats", [P, T, 6])
        mv = sb("mv", [P, T, 2])
        var_eps = sb("var_eps", [P, T])
        rstd = sb("rstd", [P, T])
        row_max = sb("row_max", [P, T])
        row_sum = sb("row_sum", [P, T])
        row_pick = sb("row_pick", [P, T])
        gate = sb("gate", [P, T])
        pick_bf = sb("pick_bf", [P, T * E], BF16)
        pick = sb("pick", [P, T, E])
        coefT = sb("coefT", [P, P])
        arena = sb("arena", [P, 14336])

        def rows(k):
            return arena[:, S * k:S * (k + 1)].rearrange("p (t d) -> p t d", d=D)

        xn, y, y1, xb, y1T = rows(0), rows(1), rows(2), rows(3), arena[:, 4 * S:5 * S]
        prod = arena[:, 10240:11264].rearrange("p (b n) -> p b n", b=2)
        pair = arena[:, 12288:13312].rearrange("p (b n) -> p b n", b=2)
        quad = arena[:, 13312:13824].rearrange("p (b n) -> p b n", b=2)
        logit = arena[:, 13824:13952].rearrange("p (t e) -> p t e", e=E)
        expo = arena[:, 13952:14080].rearrange("p (t e) -> p t e", e=E)
        coef = arena[:, 14080:14208].rearrange("p (t e) -> p t e", e=E)
        ranked = arena[:, 14208:14336].rearrange("p (t e) -> p t e", e=E)
        piece = arena[:, 0:6144].bitcast(BF16).rearrange("p (s k n) -> p s k n", s=2, k=3)
        pexp = arena[:, 6144:14336].rearrange("p (b n) -> p b n", b=2 * PB)
        rope = arena[:, 6144:10240].rearrange("p (b k n) -> p b k n", b=2, k=4)
        square = arena[:, 10240:12288].bitcast(BF16).rearrange("p (w n) -> p w n", w=2 * G)
        shift = arena[0:H, 9216:11264]
        shift_rest = arena[0:H, 11264:13312]
        shift3 = arena[0:H, 6144:9216].bitcast(BF16).rearrange("h (k n) -> h k n", k=3)
        oT = arena[:, 12288:14336]
        packed = sb("packed", [P, SETS, 2, GH, S], BF16)
        fold = packed[:].rearrange("p a b h n -> p (a b h n)").bitcast(F32)
        w1T = fold[:, 0:4096].rearrange("p (e c d) -> p e c d", e=E, c=FC)
        w2 = fold[:, 4096:8192].rearrange("p (e c d) -> p e c d", e=E, c=FC)
        b1_only = fold[:, 8192:12288].rearrange("p (c e t f) -> p c e t f", c=FC, e=E, t=T)
        b1_t = fold[:, 12288:12320].rearrange("p (c e) -> p c e", c=FC)
        e_is = fold[:, 12416:13440].rearrange("p (e t f) -> p e t f", e=E, t=T)
        b2_rep = fold[:, 13440:13568]
        wv = fold[:, 13568:13696]
        woT = fold[:, 13696:13824]
        bv = fold[:, 13824:13825]
        bv_rep = fold[:, 13952:14080]
        ob_rep = fold[:, 14080:14208]
        v_tm = sb("v_tm", [P, T, D])
        v_st = sb("v_st", [P, SETS, T, GH, VC])
        o_sb = sb("o_sb", [P, 2, GW])
        den = sb("den", [P, 2, GT, GH])
        head_of = sb("head_of", [P, H], BF16)
        half = sb("half", [H, 2])
        longest = sb("longest", [H, 2])
        ratio = sb("ratio", [H, 4])
        line = sb("line", [H, 2])
        beyond = sb("beyond", [H, 2])
        flag = sb("flag", [1, 1], I32)
        top = sb("top", [P, P])
        topT = sb("topT", [GH * T, P])
        piece_dram = nc.dram_tensor("piece_dram", [2, 3, H, HD, S], BF16).ap()
        shift_dram = nc.dram_tensor("shift_dram", [H, S], F32).ap()
        shift3_dram = nc.dram_tensor("shift3_dram", [3, H, S], BF16).ap()

        x_in = [sem(f"x_in{g}") for g in range(G)]
        w_in = [sem(f"w_in{e}") for e in range(E)]
        packed_in = [sem(f"packed_in{s}") for s in range(SETS)]
        const_in, mha_in, fold_in, att_in, rope_in, template_in = (sem(n) for n in
            ("const_in", "mha_in", "fold_in", "att_in", "rope_in", "template_in"))
        prep_pool, prep_dve, prep_act, prep_mm = (sem(n) for n in ("prep_pool", "prep_dve", "prep_act", "prep_mm"))
        ln_part, ln_stats, ln_var, ln_rstd = (sem(n) for n in ("ln_part", "ln_stats", "ln_var", "ln_rstd"))
        normed, turned, copied = sem("normed"), sem("turned"), sem("copied")
        mha_mm, mha_read, logit_mm = sem("mha_mm"), sem("mha_read"), sem("logit_mm")
        route, logit_sub, exp_ready, pick_ready, place_mm, coef_ready, coef_mm, coefT_ready = (sem(n) for n in
            ("route", "logit_sub", "exp_ready", "pick_ready", "place_mm", "coef_ready", "coef_mm", "coefT_ready"))
        y1_ready, xb_ready, bias_mm, bias_read = (sem(n) for n in ("y1_ready", "xb_ready", "bias_mm", "bias_read"))
        expert_mm, high_ready, pair_ready, quad_ready, z_ready = (sem(n) for n in
            ("expert_mm", "high_ready", "pair_ready", "quad_ready", "z_ready"))
        z_part, x_new = sem("z_part"), sem("x_new")
        proj_mm, rope_part, rotated, high_piece, rest_ready, mid_piece, low_piece = (sem(n) for n in
            ("proj_mm", "rope_part", "rotated", "high_piece", "rest_ready", "mid_piece", "low_piece"))
        v_mm, v_ready, v_staged, piece_out = (sem(n) for n in ("v_mm", "v_ready", "v_staged", "piece_out"))
        max_in, max_mm, max_read, top_mm, top_ready, top_out = (sem(n) for n in
            ("max_in", "max_mm", "max_read", "top_mm", "top_ready", "top_out"))
        squared, norm_mm, bound, root_ready, beyond_mm, flag_ready, true_shift = (sem(n) for n in
            ("squared", "norm_mm", "bound", "root_ready", "beyond_mm", "flag_ready", "true_shift"))
        shift_in, shift_ready, shift_out = (sem(n) for n in ("shift_in", "shift_ready", "shift_out"))
        score_mm, exp_done, pv_done = sem("score_mm"), sem("exp_done"), sem("pv_done")
        o_copied, o_turned, den_ready, o_read = (sem(n) for n in ("o_copied", "o_turned", "den_ready", "o_read"))
        out_mm, stored = sem("out_mm"), sem("stored")

        block = ctx.enter_context(nc.Block())

        def norm_no(n, k):
            return 4 * n + k

        def turn_no(n, k):
            return 4 * n + k

        def cols(g):
            return slice(GW * g, GW * (g + 1))

        def bank_tiles(b):
            return ps[:, b, :].rearrange("p (t d) -> p t d", d=D)

        def rows_of(v, n=GT):
            return v.unsqueeze(1).to_broadcast([P, n, D])

        SMALL = 6
        PACK_DMAS = len(Q_PIECE) + len(K_PIECE)

        @block.sync
        def _(sp):
            for g in range(G):
                sp.dma_start(x_tm[:, GT * g:GT * (g + 1), :],
                             a["x"][cols(g), :].rearrange("(t p) d -> p t d", p=P)).then_inc(x_in[g], 16)
            for dst, src in ((ident[:], a["ident"]), (tri_bf[:], a["tri"].bitcast(BF16)), (tile_is[:], a["tile_is"]),
                             (head_of[:], a["head_of"].bitcast(BF16)),
                             (rank[:], a["rank"].partition_broadcast(P)),
                             (fold[:, 12416:13440], a["e_is"].partition_broadcast(P))):
                sp.dma_start(dst, src).then_inc(const_in, 16)
            for dst, src in ((wv, a["wv"]), (woT, a["woT"]), (bv, a["bv"]), (ob_rep, a["ob"].partition_broadcast(P)),
                             (g1c[:], a["g1c"]), (lnb[:], a["lnb"].partition_broadcast(P)), (wg[:], a["wg"])):
                sp.dma_start(dst, src).then_inc(mha_in, 16)
            sp.dma_start(b1_t, a["b1_t"]).then_inc(fold_in, 16)
            sp.dma_start(b2_rep, a["b2_rep"]).then_inc(fold_in, 16)
            for e in range(E):
                sp.dma_start(w1T[:, e, :, :], a["w1T"][e].rearrange("(p c) d -> p c d", c=FC)).then_inc(w_in[e], 16)
                sp.dma_start(w2[:, e, :, :], a["w2"][e].rearrange("(p c) d -> p c d", c=FC)).then_inc(w_in[e], 16)
            for dst, src in ((wqo[:, 0, :], a["wq"]), (wqo[:, 1, :], a["wo"]), (wdu[:, 0, :], a["w_downT"]),
                             (wdu[:, 1, :], a["wk_up"]), (wdu[:, 2, :], a["wv_up"])):
                sp.dma_start(dst, src).then_inc(att_in, 16)
            for i, dst in enumerate((cos, sin)):
                sp.dma_start(dst, a["rope"][i]).then_inc(rope_in, 16)
            sp.wait_ge(prep_mm, PREP_MM)
            sp.wait_ge(prep_dve, PREP_DVE)
            for s in range(SETS):
                for side in range(2):
                    src = a["template"][side].bitcast(BF16).unsqueeze(1).to_broadcast([P - SHIFT_ROW, GH, S])
                    sp.dma_start(packed[SHIFT_ROW:P, s, side, :, :], src).then_inc(template_in, 16)
            for g in range(G):
                for side in range(2):
                    sp.wait_ge(low_piece, 2 * g + side + 1)
                    dst = piece_dram[side, :, :, :, cols(g)].rearrange("k h d n -> (h d) k n")
                    sp.dma_start(dst, piece[:, side, :, cols(g)]).then_inc(piece_out, 16)
            sp.wait_ge(piece_out, 16 * 2 * G)
            sp.wait_ge(template_in, 16 * SETS * 2)

            def load_packed(s, first_head, done):
                for side, pieces in enumerate((Q_PIECE, K_PIECE)):
                    for b, k in enumerate(pieces):
                        src = piece_dram[side, k, bass.ds(first_head, GH), :, :].rearrange("h d n -> d h n")
                        sp.dma_start(packed[HD * b:HD * (b + 1), s, side, :, :], src).then_inc(done, 16)

            for g in range(SETS):
                load_packed(g, g * GH, packed_in[g])
            sp.wait_ge(flag_ready, 1)
            beyond_safe = sp.value_load(flag[0:1, 0:1], min_val=0, max_val=H)
            with sp.If(beyond_safe > 0):
                sp.wait_ge(packed_in[0], 16 * PACK_DMAS)
                sp.sem_inc(top_out, 16)
                with sp.Fori(0, NG) as g:
                    sp.wait_ge(top_mm, g + 1)
                    load_packed(0, g * GH, max_in)
                    sp.wait_ge(top_ready, g + 2)
                    dst = shift_dram[bass.ds(g * GH, GH), :].rearrange("h (t p) -> (h t) p", p=P)
                    sp.dma_start(dst, topT[:, :]).then_inc(top_out, 16)
                sp.wait_ge(top_out, 16 + 16 * NG)
                sp.dma_start(shift, shift_dram[:, :]).then_inc(shift_in, 16)
                sp.wait_ge(top_mm, 1 + NG)
                load_packed(0, 0, max_in)
                sp.wait_ge(max_in, 16 * PACK_DMAS * (NG + 1))
            sp.wait_ge(shift_ready, 1)
            sp.dma_start(shift3_dram.rearrange("k h n -> h k n"), shift3).then_inc(shift_out, 16)
            sp.wait_ge(shift_out, 16)
            for g in range(NG):
                if g >= SETS:
                    sp.wait_ge(score_mm, (g - SETS + 1) * NE // SETS)
                    load_packed(g % SETS, g * GH, packed_in[g % SETS])
                sp.dma_start(packed[SHIFT_ROW:SHIFT_ROW + 3, g % SETS, 0, :, :],
                             shift3_dram[:, GH * g:GH * (g + 1), :]).then_inc(packed_in[g % SETS], 16)
            for g in range(G):
                sp.wait_ge(x_new, 2 * G + g + 1)
                sp.dma_start(out[cols(g), :].rearrange("(t p) d -> p t d", p=P),
                             x_tm[:, GT * g:GT * (g + 1), :]).then_inc(stored, 16)
            sp.wait_ge(stored, 16 * G)

        @block.gpsimd
        def _(pool):
            def ln_rsqrt(no, g):
                pool.wait_ge(ln_stats, G * no + g + 1)
                pool.tensor_scalar(var_eps[:, GT * g:GT * (g + 1)], mv[:, GT * g:GT * (g + 1), 1], EPS, None, ALU.add).then_inc(ln_var, 1)
                pool.wait_ge(ln_var, G * no + g + 1)
                pool.tensor_tensor(rstd[:, GT * g:GT * (g + 1)], var_eps[:, GT * g:GT * (g + 1)], neg_half[:],
                                   ALU.pow).then_inc(ln_rstd, 1)

            pool.memset(neg_half[:], -0.5).then_inc(prep_pool, 1)
            pool.wait_ge(prep_pool, 1)
            for g in range(G):
                ln_rsqrt(norm_no(0, 0), g)
            pool.wait_ge(mha_in, 16 * 7)
            pool.tensor_scalar(lnb[:, 2:4, :], lnb[:, 2:4, :], 0.5, None, ALU.mult).then_inc(prep_pool, 1)
            pool.wait_ge(const_in, 16 * SMALL)
            pool.wait_ge(fold_in, 16 * 2)
            for c in range(FC):
                pool.tensor_tensor(b1_only[:, c, :, :, :].rearrange("p e t f -> p e (t f)"),
                                   b1_t[:, c, :].unsqueeze(2).to_broadcast([P, E, T * E]),
                                   e_is.rearrange("p e t f -> p e (t f)"), ALU.mult).then_inc(prep_pool, 1)

            def feed_forward(n):
                if n:
                    for g in range(G):
                        ln_rsqrt(norm_no(n, 0), g)
                pool.wait_ge(prep_pool, 2)
                for g in range(G):
                    t = slice(GT * g, GT * (g + 1))
                    if n == 0:
                        pool.wait_ge(x_in[g], 16)
                    pool.tensor_tensor(xb[:, t, :], x_tm[:, t, :], rows_of(lnb[:, 3, :]), ALU.add).then_inc(xb_ready, 1)
                for g in range(G):
                    ln_rsqrt(norm_no(n, 1), g)
                for g in range(G):
                    t = slice(GT * g, GT * (g + 1))
                    pool.wait_ge(normed, G * (3 * n + 1) + g + 1)
                    pool.tensor_tensor(y1[:, t, :], y[:, t, :], rows_of(lnb[:, 0, :]), ALU.mult).then_inc(y1_ready, 1)
                    pool.wait_ge(y1_ready, 2 * (G * n + g) + 1)
                    pool.tensor_tensor(y1[:, t, :], y1[:, t, :], rows_of(lnb[:, 1, :]), ALU.add).then_inc(y1_ready, 1)
                if n == 0:
                    pool.wait_ge(prep_dve, 4)
                    pool.tensor_tensor(b12_big[:], b12[:].unsqueeze(1).to_broadcast([P, T, D]),
                                       tile_is[:].unsqueeze(2).to_broadcast([P, T, D]), ALU.mult).then_inc(prep_pool, 1)
                for t in range(T):
                    k = T * n + t
                    pool.wait_ge(pair_ready, k + 1)
                    if t >= 2:
                        pool.wait_ge(z_ready, k - 1)
                    q = quad[:, t % 2, :]
                    pool.tensor_tensor(q, pair[:, t % 2, 0:2 * D], pair[:, t % 2, 2 * D:4 * D],
                                       ALU.add).then_inc(quad_ready, 1)
                    pool.wait_ge(quad_ready, 2 * k + 1)
                    pool.tensor_tensor(q[:, 0:D], q[:, 0:D], q[:, D:2 * D], ALU.add).then_inc(quad_ready, 1)
                    pool.wait_ge(quad_ready, 2 * k + 2)
                    if t % GT == 0:
                        pool.wait_ge(bias_read, G * n + t // GT + 1)
                    pool.tensor_tensor(y[:, t, :], q[:, 0:D], y1[:, t, :], ALU.add).then_inc(z_ready, 1)
                    if t >= 5 and t % GT == 1:
                        ln_rsqrt(norm_no(n, 2), t // GT - 1)
                ln_rsqrt(norm_no(n, 2), G - 1)

            feed_forward(0)
            for g in range(G):
                ln_rsqrt(norm_no(0, 3), g)
            pool.memset(v_st[:], 1.0).then_inc(v_staged, 1)
            pool.memset(half[:, 0:1], 0.5).then_inc(root_ready, 1)
            pool.memset(half[:, 1:2], -0.5).then_inc(root_ready, 1)
            for w in range(2 * G):
                pool.wait_ge(rope_part, 2 * w + 2)
                if w >= 2:
                    pool.wait_ge(rest_ready, w - 1)
                    pool.wait_ge(squared, w - 1)
                pool.tensor_tensor(rope[:, w % 2, 2, :], rope[:, w % 2, 0, :], rope[:, w % 2, 1, :],
                                   ALU.add).then_inc(rotated, 1)
            pool.wait_ge(root_ready, 2)
            pool.wait_ge(bound, 6)
            pool.tensor_tensor(ratio[:, 2:4], ratio[:, 1:2].to_broadcast([H, 2]), half[:], ALU.pow).then_inc(root_ready, 1)
            pool.wait_ge(v_ready, G)
            pool.wait_ge(v_staged, 1)
            for g in range(NG):
                if g >= SETS:
                    pool.wait_ge(pv_done, PB + (g - SETS + 1) * NB // SETS)
                pool.tensor_copy(v_st[:, g % SETS, :, :, 0:HD],
                                 v_tm[:, :, GH * HD * g:GH * HD * (g + 1)].rearrange("p t (h d) -> p t h d", d=HD)
                                 ).then_inc(v_staged, 1)
            feed_forward(1)

        @block.scalar
        def _(act):
            def copy_turned(no, g, bank, dst):
                act.wait_ge(turned, G * no + g + 1)
                nc.scalar.activation(dst[:, cols(g)], ps[:, bank, :], ACT.Copy).then_inc(copied, 1)

            def feed_forward(n):
                for g in range(G):
                    copy_turned(turn_no(n, 0), g, g % 2, xT)
                if n == 0:
                    act.wait_ge(mha_in, 16 * 7)
                for g in range(G):
                    act.wait_ge(turned, G * turn_no(n, 1) + g + 1)
                    nc.scalar.activation(y1T[:, cols(g)], ps[:, 4 + g % 2, :], ACT.Identity,
                                         bias=g1c[:, 1:2], scale=g1c[:, 0:1]).then_inc(copied, 1)
                act.wait_ge(logit_sub, n + 1)
                nc.scalar.activation(expo, logit, ACT.Exp).then_inc(exp_ready, 1)
                if n == 0:
                    for b in range(2):
                        act.wait_ge(prep_mm, 3 + b)
                        nc.scalar.activation(w12[:, 512 * b:512 * (b + 1)], ps[:, b, :], ACT.Copy).then_inc(prep_act, 1)
                act.wait_ge(coef_mm, n + 1)
                nc.scalar.activation(coefT[:], ps[:, 2, 0:P], ACT.Copy).then_inc(coefT_ready, 1)
                for t in range(T):
                    k = T * n + t
                    act.wait_ge(expert_mm, k + 1)
                    act.wait_ge(coef_ready, n + 1)
                    if t >= 2:
                        act.wait_ge(pair_ready, k - 1)
                    for e in range(E // 2, E):
                        ins = nc.scalar.activation(prod[:, t % 2, D * (e - E // 2):D * (e - E // 2 + 1)],
                                                   ps[:, 2 * (t % 3) + 1, D * (e - E // 2):D * (e - E // 2 + 1)],
                                                   ACT.Copy, scale=coef[:, t, e:e + 1])
                    ins.then_inc(high_ready, 1)

            feed_forward(0)
            for g in range(G):
                copy_turned(2, g, 6 + g % 2, xT)
            for w in range(2 * G + 1):
                if w < 2 * G:
                    act.wait_ge(rotated, w + 1)
                    nc.scalar.activation(piece[:, w % 2, 0, cols(w // 2)], rope[:, w % 2, 2, :],
                                         ACT.Copy).then_inc(high_piece, 1)
                    nc.scalar.activation(square[:, w, :], rope[:, w % 2, 2, :], ACT.Square).then_inc(squared, 1)
                if w >= 1:
                    act.wait_ge(rest_ready, w)
                    nc.scalar.activation(piece[:, (w - 1) % 2, 1, cols((w - 1) // 2)], rope[:, (w - 1) % 2, 3, :],
                                         ACT.Copy).then_inc(mid_piece, 1)
            for g in range(G):
                act.wait_ge(v_mm, g + 1)
                nc.scalar.activation(v_tm[:, GT * g:GT * (g + 1), :], bank_tiles(g), ACT.Copy).then_inc(v_ready, 1)
            act.sem_inc(exp_done, EB)
            with act.Fori(0, NG // SETS) as i:
                for n in range(NE):
                    act.wait_ge(score_mm, i * NE + n + 1)
                    if n % 2 == 0:
                        act.wait_ge(pv_done, i * NB + n // 2 + 1)
                    src = ps[:, 2 * (n % EB):2 * (n % EB) + 2, :].rearrange("p b n -> p (b n)")
                    nc.scalar.activation(pexp[:, 2 * (n // 2 % PB) + n % 2, :], src, ACT.Exp,
                                         scale=SCALE).then_inc(exp_done, 1)
            for g in range(G):
                copy_turned(3, g, g % 2, oT)
            feed_forward(1)

        @block.vector
        def _(dve):
            def ln_stats_of(no, g, src):
                for t in range(GT * g, GT * (g + 1)):
                    ins = dve.bn_stats(stats[:, t, :], src[:, t, :])
                ins.then_inc(ln_part, 1)
                dve.wait_ge(ln_part, G * no + g + 1)
                for t in range(GT * g, GT * (g + 1)):
                    ins = dve.bn_aggr(mv[:, t, :], stats[:, t, :])
                ins.then_inc(ln_stats, 1)

            def normalise(no, turn, g, src, dst):
                dve.wait_ge(ln_stats, G * no + g + 1)
                dve.wait_ge(ln_rstd, G * no + g + 1)
                for t in range(GT * g, GT * (g + 1)):
                    ins = dve.tensor_scalar(dst[:, t, :], src[:, t, :], mv[:, t, 0:1], rstd[:, t:t + 1],
                                            ALU.subtract, ALU.mult)
                ins.then_inc(normed, 1)
                assert turn is not None

            def feed_forward(n):
                for g in range(G):
                    if n == 0:
                        dve.wait_ge(x_in[g], 16)
                    else:
                        dve.wait_ge(x_new, G + g + 1)
                    ln_stats_of(norm_no(n, 0), g, x_tm)
                for g in range(G):
                    normalise(norm_no(n, 0), turn_no(n, 0), g, x_tm, xn)
                if n == 0:
                    dve.wait_ge(mha_in, 16 * 7)
                    dve.tensor_copy(bv_rep, bv.to_broadcast([P, D])).then_inc(prep_dve, 1)
                    dve.wait_ge(const_in, 16 * SMALL)
                    dve.wait_ge(prep_mm, 2)
                    dve.tensor_tensor(w_mha[:], ps[:, 7, 0:D], ident[:], ALU.add).then_inc(prep_dve, 1)
                    dve.tensor_tensor(b_mha[:], ps[:, 7, D:2 * D], ob_rep, ALU.add).then_inc(prep_dve, 1)
                    dve.wait_ge(prep_dve, 3)
                for g in range(G):
                    t = slice(GT * g, GT * (g + 1))
                    dve.wait_ge(mha_mm, G * n + g + 1)
                    dve.tensor_tensor(y[:, t, :], bank_tiles(2 + g % 2), rows_of(b_mha[:]), ALU.add).then_inc(mha_read, 1)
                    dve.wait_ge(mha_read, G * n + g + 1)
                    ln_stats_of(norm_no(n, 1), g, y)
                for g in range(G):
                    normalise(norm_no(n, 1), turn_no(n, 1), g, y, y)
                lg = ps[:, 6, 0:T * E].rearrange("p (t e) -> p t e", e=E)

                def over_experts(v):
                    return v.unsqueeze(2).to_broadcast([P, T, E])

                dve.wait_ge(logit_mm, G * n + G)
                dve.tensor_reduce(row_max[:], lg, AX, ALU.max).then_inc(route, 1)
                dve.wait_ge(route, 5 * n + 1)
                dve.tensor_tensor(logit, lg, over_experts(row_max[:]), ALU.subtract).then_inc(logit_sub, 1)
                if n == 0:
                    dve.wait_ge(prep_mm, 5)
                    dve.tensor_tensor(b12[:], ps[:, 3, 0:D], b2_rep, ALU.add).then_inc(prep_dve, 1)
                    dve.wait_ge(prep_mm, 6)
                    dve.tensor_copy(wkv[:].rearrange("p a d -> p (a d)"), ps[:, 4, 0:2 * D]).then_inc(prep_dve, 1)
                dve.wait_ge(exp_ready, n + 1)
                dve.tensor_reduce(row_sum[:], expo, AX, ALU.add).then_inc(route, 1)
                dve.scalar_tensor_tensor(ranked, expo, 1.0, rank[:], ALU.is_ge, ALU.mult).then_inc(route, 1)
                dve.wait_ge(route, 5 * n + 3)
                dve.reciprocal(gate[:], row_sum[:]).then_inc(route, 1)
                dve.tensor_reduce(row_pick[:], ranked, AX, ALU.max).then_inc(route, 1)
                dve.wait_ge(route, 5 * n + 5)
                dve.tensor_tensor(pick_bf[:].rearrange("p (t e) -> p t e", e=E), ranked, over_experts(row_pick[:]),
                                  ALU.is_equal).then_inc(pick_ready, 1)
                dve.tensor_tensor(pick[:], ranked, over_experts(row_pick[:]), ALU.is_equal).then_inc(pick_ready, 1)
                dve.wait_ge(place_mm, n + 1)
                dve.wait_ge(pick_ready, 2 * n + 2)
                place = ps[:, 7, 0:T * E].rearrange("p (t e) -> p t e", e=E)
                dve.scalar_tensor_tensor(pick[:], place, float(CAP), pick[:], ALU.is_le, ALU.mult).then_inc(z_part, 1)
                dve.wait_ge(z_part, 1 + n * (1 + G))
                dve.tensor_tensor(coef, pick[:], over_experts(gate[:]), ALU.mult).then_inc(coef_ready, 1)
                dve.wait_ge(coef_ready, n + 1)

                def stats_z(g):
                    dve.wait_ge(z_ready, T * n + GT * (g + 1))
                    ln_stats_of(norm_no(n, 2), g, y)

                def finish(g):
                    dve.wait_ge(ln_stats, G * norm_no(n, 2) + g + 1)
                    for t in range(GT * g, GT * (g + 1)):
                        ins = dve.scalar_tensor_tensor(y[:, t, :], y[:, t, :], mv[:, t, 0:1], lnb[:, 2, :],
                                                       ALU.subtract, ALU.mult)
                    ins.then_inc(z_part, 1)
                    dve.wait_ge(z_part, n * (1 + G) + 1 + g + 1)
                    dve.wait_ge(ln_rstd, G * norm_no(n, 2) + g + 1)
                    dve.wait_ge(xb_ready, G * n + g + 1)
                    for t in range(GT * g, GT * (g + 1)):
                        ins = dve.scalar_tensor_tensor(x_tm[:, t, :], y[:, t, :], rstd[:, t:t + 1], xb[:, t, :],
                                                       ALU.mult, ALU.add)
                    ins.then_inc(x_new, 1)

                for t in range(T):
                    k, g = T * n + t, t // GT
                    if t % GT == 0:
                        dve.wait_ge(bias_mm, G * n + g + 1)
                        dve.wait_ge(y1_ready, 2 * (G * n + g) + 2)
                        tt = slice(t, t + GT)
                        dve.tensor_tensor(y1[:, tt, :], y1[:, tt, :], bank_tiles(6 + g % 2), ALU.add).then_inc(bias_read, 1)
                    dve.wait_ge(expert_mm, k + 1)
                    dve.wait_ge(high_ready, k + 1)
                    if t >= 2:
                        dve.wait_ge(quad_ready, 2 * (k - 2) + 1)
                    for e in range(E // 2):
                        ins = dve.scalar_tensor_tensor(pair[:, t % 2, D * e:D * (e + 1)],
                                                       ps[:, 2 * (t % 3), D * e:D * (e + 1)], coef[:, t, e:e + 1],
                                                       prod[:, t % 2, D * e:D * (e + 1)], ALU.mult, ALU.add)
                    ins.then_inc(pair_ready, 1)
                    if t >= 5 and t % GT == 1:
                        stats_z(g - 1)
                    if t >= 7 and t % GT == 3:
                        finish(g - 1)
                stats_z(G - 1)
                finish(G - 1)

            feed_forward(0)

            for g in range(G):
                dve.wait_ge(x_new, g + 1)
                ln_stats_of(norm_no(0, 3), g, x_tm)
            for g in range(G):
                normalise(norm_no(0, 3), 2, g, x_tm, xn)
            dve.wait_ge(att_in, 16 * 5)
            for k, w in enumerate((wqo[:, 0, :], wkv[:, 0, :])):
                even_odd = w.rearrange("p (n two) -> p n two", two=2)
                to = wsw[:, k, :].rearrange("p (n two) -> p n two", two=2)
                dve.tensor_scalar(to[:, :, 0], even_odd[:, :, 1], -1.0, None, ALU.mult).then_inc(prep_dve, 1)
                dve.tensor_copy(to[:, :, 1], even_odd[:, :, 0]).then_inc(prep_dve, 1)
            dve.wait_ge(rope_in, 16 * 2)
            for w in range(2 * G + 2):
                if w < 2 * G:
                    g, side = w // 2, w % 2
                    dve.wait_ge(proj_mm, w + 1)
                    if w >= 2:
                        dve.wait_ge(rotated, w - 1)
                    for k, table in enumerate((cos, sin)):
                        dve.tensor_tensor(rope[:, w % 2, k, :], ps[:, 4 * (g % 2) + 2 * side + k, :],
                                          table[:, cols(g)], ALU.mult).then_inc(rope_part, 1)
                if 1 <= w <= 2 * G:
                    v = w - 1
                    dve.wait_ge(high_piece, v + 1)
                    if v >= 2:
                        dve.wait_ge(low_piece, v - 1)
                    dve.tensor_tensor(rope[:, v % 2, 3, :], rope[:, v % 2, 2, :], piece[:, v % 2, 0, cols(v // 2)],
                                      ALU.subtract).then_inc(rest_ready, 1)
                if w >= 2:
                    v = w - 2
                    dve.wait_ge(mid_piece, v + 1)
                    dve.tensor_tensor(piece[:, v % 2, 2, cols(v // 2)], rope[:, v % 2, 3, :],
                                      piece[:, v % 2, 1, cols(v // 2)], ALU.subtract).then_inc(low_piece, 1)

            norms = [ps[0:H, 4 * b:4 * b + 4, :].rearrange("h b n -> h (b n)") for b in (1, 0)]
            for side in range(2):
                dve.wait_ge(norm_mm, side + 1)
                dve.tensor_reduce(longest[:, side:side + 1], norms[side], AX, ALU.max).then_inc(bound, 1)
            dve.wait_ge(bound, 2)
            dve.tensor_scalar(longest[:], longest[:], 1e-12, None, ALU.max).then_inc(bound, 1)
            dve.wait_ge(bound, 3)
            dve.reciprocal(ratio[:, 0:1], longest[:, 0:1]).then_inc(bound, 1)
            dve.tensor_tensor(beyond[:, 0:1], longest[:, 0:1], longest[:, 1:2], ALU.mult).then_inc(bound, 1)
            dve.wait_ge(bound, 5)
            dve.tensor_tensor(ratio[:, 1:2], ratio[:, 0:1], longest[:, 1:2], ALU.mult).then_inc(bound, 1)
            dve.tensor_scalar(beyond[:, 1:2], beyond[:, 0:1], (SAFE / SCALE) ** 2, None, ALU.is_le).then_inc(bound, 1)
            dve.memset(shift3[:, 1:3, :], 0.0).then_inc(bound, 1)
            dve.wait_ge(root_ready, 3)
            dve.tensor_scalar(line[:, 0:1], ratio[:, 2:3], -0.51, None, ALU.mult).then_inc(bound, 1)
            dve.tensor_scalar(line[:, 1:2], longest[:, 1:2], ratio[:, 3:4], -0.51, ALU.mult, ALU.mult).then_inc(bound, 1)
            dve.wait_ge(bound, 10)
            dve.tensor_scalar(shift3[:, 0, :], norms[0], line[:, 0:1], line[:, 1:2], ALU.mult, ALU.add).then_inc(bound, 1)
            dve.tensor_scalar(beyond[:, 1:2], beyond[:, 1:2], -1.0, 1.0, ALU.mult, ALU.add).then_inc(bound, 1)
            dve.wait_ge(bound, 11)
            dve.wait_ge(beyond_mm, 1)
            dve.tensor_scalar(flag[:], ps[0:1, 0, 0:1], -2.0, None, ALU.mult).then_inc(flag_ready, 1)
            dve.wait_ge(flag_ready, 1)
            beyond_safe = dve.value_load(flag[0:1, 0:1], min_val=0, max_val=H)
            with dve.If(beyond_safe > 0):
                dve.memset(top[:, GH * T:P], 0.0).then_inc(max_read, 2)
                dve.sem_inc(top_ready, 1)
                with dve.Fori(0, NG) as gg:
                    for m in range(GH * T):
                        t = m % T
                        dve.wait_ge(max_mm, gg * (GH * T) + m + 1)
                        flat = ps[:, 4 * (m % 2):4 * (m % 2) + 4, :].rearrange("p b n -> p (b n)")
                        dve.tensor_reduce(top[:, m:m + 1], flat[:, 0:P * (t + 1)], AX, ALU.max).then_inc(max_read, 1)
                    dve.wait_ge(top_mm, gg + 2)
                    dve.wait_ge(top_out, gg * 16 + 16)
                    dve.tensor_scalar(topT[:], ps[0:GH * T, 0, 0:P], -1.0, None, ALU.mult).then_inc(top_ready, 1)
                dve.wait_ge(shift_in, 16)
                dve.tensor_copy(shift3[:, 0, :], shift).then_inc(true_shift, 1)
                dve.wait_ge(true_shift, 1)
                dve.tensor_tensor(shift_rest, shift, shift3[:, 0, :], ALU.subtract).then_inc(true_shift, 1)
                dve.wait_ge(true_shift, 2)
                dve.tensor_copy(shift3[:, 1, :], shift_rest).then_inc(true_shift, 1)
                dve.wait_ge(true_shift, 3)
                dve.tensor_tensor(shift3[:, 2, :], shift_rest, shift3[:, 1, :], ALU.subtract).then_inc(true_shift, 1)
                dve.wait_ge(true_shift, 4)
            dve.sem_inc(shift_ready, 1)

            dve.sem_inc(o_read, OB)
            with dve.Fori(0, NG // SETS) as i:
                for s in range(SETS):
                    for c in range(G):
                        no = i * (SETS * G) + (s * G + c)
                        b = c % OB
                        dve.wait_ge(pv_done, i * NB + (PB + s * (NB // SETS) + CHUNK_END[c] + 1))
                        dve.tensor_copy(o_sb[:, b, :], ps[:, 6 + b, :]).then_inc(o_copied, 1)
                        dve.wait_ge(o_turned, no + 1)
                        turned_o = ps[:, 6 + b, :].rearrange("p (t h v) -> p t h v", h=GH, v=VC)
                        dve.reciprocal(den[:, b, :, :], turned_o[:, :, :, HD]).then_inc(den_ready, 1)
                        dve.wait_ge(den_ready, no + 1)
                        dst = attn_tm[:, GT * c:GT * (c + 1), bass.ds(i * (SETS * GH * HD) + s * GH * HD, GH * HD)]
                        dve.tensor_tensor(dst.rearrange("p t (h d) -> p t h d", d=HD), turned_o[:, :, :, 0:HD],
                                          den[:, b, :, :].unsqueeze(3).to_broadcast([P, GT, GH, HD]),
                                          ALU.mult).then_inc(o_read, 1)
            for g in range(G):
                t = slice(GT * g, GT * (g + 1))
                dve.wait_ge(out_mm, g + 1)
                dve.tensor_tensor(x_tm[:, t, :], x_tm[:, t, :], bank_tiles(2 + g % 2), ALU.add).then_inc(x_new, 1)
            feed_forward(1)

        @block.tensor
        def _(pe):
            def turn(no, g, bank, src, free=None):
                pe.wait_ge(normed, G * (no - (no > 3)) + g + 1)
                if g >= 2:
                    pe.wait_ge(copied, G * no + g - 1)
                for k in range(GT):
                    ins = pe.transpose(ps[:, bank, P * k:P * (k + 1)], src[:, GT * g + k, :], ident[:])
                ins.then_inc(turned, 1)

            def by_tile(bank, g, lhs, rhs, done):
                for k in range(GT):
                    n = P * (GT * g + k)
                    ins = pe.matmul(ps[:, bank, D * k:D * (k + 1)], lhs[:, n:n + P], rhs, start=True, stop=True)
                ins.then_inc(done, 1)

            def feed_forward(n):
                if n == 0:
                    pe.wait_ge(const_in, 16 * SMALL)
                for g in range(G + 1):
                    if g < G:
                        turn(turn_no(n, 0), g, g % 2, xn)
                    if g == 0 and n == 0:
                        pe.wait_ge(mha_in, 16 * 7)
                        pe.matmul(ps[:, 7, 0:D], wv, woT, start=True, stop=True).then_inc(prep_mm, 1)
                        pe.wait_ge(prep_dve, 1)
                        pe.matmul(ps[:, 7, D:2 * D], bv_rep, woT, start=True, stop=True).then_inc(prep_mm, 1)
                        pe.wait_ge(prep_dve, 2)
                    if g >= 1:
                        pe.wait_ge(copied, G * turn_no(n, 0) + g)
                        if g >= 3:
                            pe.wait_ge(mha_read, G * n + g - 2)
                        by_tile(2 + (g - 1) % 2, g - 1, xT, w_mha[:], mha_mm)
                for g in range(G):
                    turn(turn_no(n, 1), g, 4 + g % 2, y)
                for g in range(G):
                    pe.wait_ge(copied, G * turn_no(n, 1) + g + 1)
                    for k in range(GT):
                        t = GT * g + k
                        ins = pe.matmul(ps[:, 6, E * t:E * (t + 1)], y1T[:, P * t:P * (t + 1)], wg[:],
                                        start=True, stop=True)
                    ins.then_inc(logit_mm, 1)
                if n == 0:
                    pe.wait_ge(mha_read, G)
                    pe.wait_ge(prep_pool, 2 + FC)
                    for e in range(E):
                        pe.wait_ge(w_in[e], 32)
                        for c in range(FC):
                            ins = pe.matmul(ps[:, e // 4, D * (e % 4):D * (e % 4 + 1)], w1T[:, e, c, :], w2[:, e, c, :],
                                            start=(c == 0), stop=(c == FC - 1))
                        if e % 4 == 3:
                            ins.then_inc(prep_mm, 1)
                    for e in range(E):
                        for c in range(FC):
                            ins = pe.matmul(ps[:, 3, 0:D], b1_only[:, c, e, :, :].rearrange("p t f -> p (t f)"),
                                            w2[:, e, c, :], start=(e + c == 0), stop=(e == E - 1 and c == FC - 1))
                    ins.then_inc(prep_mm, 1)
                    pe.wait_ge(att_in, 16 * 5)
                    for k in range(2):
                        ins = pe.matmul(ps[:, 4, D * k:D * (k + 1)], wdu[:, 0, :], wdu[:, 1 + k, :], start=True, stop=True)
                    ins.then_inc(prep_mm, 1)
                pe.wait_ge(pick_ready, 2 * n + 1)
                if n == 0:
                    pe.wait_ge(prep_dve, 3)
                pe.matmul(ps[:, 7, 0:T * E], tri_bf[:, 0, :], pick_bf[:], start=True, stop=False)
                for back in range(1, T):
                    ins = pe.matmul(ps[:, 7, E * back:T * E], tri_bf[:, 1, :], pick_bf[:, 0:E * (T - back)],
                                    start=False, stop=(back == T - 1))
                ins.then_inc(place_mm, 1)
                pe.wait_ge(coef_ready, n + 1)
                pe.transpose(ps[:, 2, 0:P], coef.rearrange("p t e -> p (t e)"), ident[:]).then_inc(coef_mm, 1)
                pe.wait_ge(coefT_ready, n + 1)
                if n == 0:
                    pe.wait_ge(prep_pool, 3 + FC)
                    pe.wait_ge(prep_act, 2)
                    pe.wait_ge(prep_dve, 5)
                for t in range(T):
                    k, g = T * n + t, t // GT
                    if t % GT == 0:
                        if g >= 2:
                            pe.wait_ge(bias_read, G * n + g - 1)
                        for j in range(GT):
                            ins = pe.matmul(ps[:, 6 + g % 2, D * j:D * (j + 1)], coefT[:], b12_big[:, t + j, :],
                                            start=True, stop=True)
                        ins.then_inc(bias_mm, 1)
                    if t >= 3:
                        pe.wait_ge(pair_ready, k - 2)
                        pe.wait_ge(high_ready, k - 2)
                    for b in range(2):
                        ins = pe.matmul(ps[:, 2 * (t % 3) + b, :], y1T[:, P * t:P * (t + 1)],
                                        w12[:, 512 * b:512 * (b + 1)], start=True, stop=True)
                    ins.then_inc(expert_mm, 1)

            feed_forward(0)

            for g in range(G):
                turn(2, g, 6 + g % 2, xn)
            pe.wait_ge(prep_dve, 9)
            for w in range(2 * G):
                g, side = w // 2, w % 2
                pe.wait_ge(copied, G * 2 + (g + 1 if g == 0 else G))
                if g >= 2:
                    pe.wait_ge(rope_part, 2 * (w - 4) + 2)
                for k, lhs in enumerate(((wqo[:, 0, :], wsw[:, 0, :]), (wkv[:, 0, :], wsw[:, 1, :]))[side]):
                    ins = pe.matmul(ps[:, 4 * (g % 2) + 2 * side + k, :], lhs, xT[:, cols(g)], start=True, stop=True)
                ins.then_inc(proj_mm, 1)
            pe.wait_ge(rope_part, 2 * 6)
            for g in range(G):
                by_tile(g, g, xT, wkv[:, 1, :], v_mm)

            pe.wait_ge(squared, 2 * G)
            pe.wait_ge(rope_part, 2 * 2 * G)
            for side in range(2):
                if side:
                    pe.wait_ge(v_ready, G)
                for g in range(G):
                    ins = pe.matmul(ps[0:H, 4 * (1 - side) + g, :], head_of[:], square[:, 2 * g + side, :],
                                    start=True, stop=True)
                ins.then_inc(norm_mm, 1)
            pe.wait_ge(bound, 12)
            pe.matmul(ps[0:1, 0, 0:1], beyond[:, 1:2], neg_half[0:H, 0:1], start=True, stop=True).then_inc(beyond_mm, 1)
            pe.wait_ge(flag_ready, 1)
            beyond_safe = pe.value_load(flag[0:1, 0:1], min_val=0, max_val=H)
            with pe.If(beyond_safe > 0):
                pe.sem_inc(top_mm, 1)
                with pe.Fori(0, NG) as gg:
                    pe.wait_ge(max_in, gg * (16 * PACK_DMAS) + 16 * PACK_DMAS)
                    pe.wait_ge(top_ready, gg + 1)
                    for m in range(GH * T):
                        h, t = m // T, m % T
                        pe.wait_ge(max_read, gg * (GH * T) + m + 1)
                        for n in range(0, P * (t + 1), 512):
                            w = min(512, P * (t + 1) - n)
                            ins = pe.matmul(ps[:, 4 * (m % 2) + n // 512, 0:w], packed[:, 0, 0, h, P * t:P * (t + 1)],
                                            packed[:, 0, 1, h, n:n + w], start=True, stop=True)
                        ins.then_inc(max_mm, 1)
                    pe.wait_ge(max_read, gg * (GH * T) + GH * T + 2)
                    pe.transpose(ps[:, 0, 0:P], top[:], ident[:]).then_inc(top_mm, 1)
                pe.wait_ge(top_ready, 1 + NG)

            pe.sem_inc(pv_done, PB)
            with pe.Fori(0, NG // SETS) as i:
                def scores(n):
                    s, first = n // (NE // SETS), 2 * (n % (NE // SETS))
                    if first == 0:
                        pe.wait_ge(packed_in[s], i * (16 * (PACK_DMAS + 1)) + 16 * (PACK_DMAS + 1))
                    pe.wait_ge(exp_done, i * NE + (EB + previous_exp(n) + 1))
                    for b in range(2):
                        for h, j, q, w, col in BANKS[first + b]:
                            ins = pe.matmul(ps[:, 2 * (n % EB) + b, col:col + w], packed[:, s, 1, h, P * j:P * (j + 1)],
                                            packed[:, s, 0, h, q:q + w], start=True, stop=True)
                    ins.then_inc(score_mm, 1)

                def values(m):
                    s, first = m // (NB // SETS), 4 * (m % (NB // SETS))
                    if first == 0:
                        pe.wait_ge(v_staged, i * SETS + s + 2)
                    pe.wait_ge(exp_done, i * NE + (EB + 2 * m + 2))
                    for b in range(4):
                        for h, j, q, w, col in BANKS[first + b]:
                            c = chunk_of((h, j, q, w, col))
                            if j == 0 and h == 0:
                                pe.wait_ge(o_read, i * (SETS * G) + (s * G + c + 1))
                            last = j == GT * c + 2
                            ins = pe.matmul(ps[32 * h:32 * h + VC, 6 + c % OB, q - GW * c:q - GW * c + w],
                                            v_st[:, s, j, h, :], pexp[:, 2 * (m % PB) + b // 2, 512 * (b % 2) + col:512 * (b % 2) + col + w],
                                            start=(j == 0), stop=last, tile_position=(0, 32 * h), skip_group_check=True)
                    ins.then_inc(pv_done, 1)

                def turn_output(k):
                    pe.wait_ge(o_copied, i * (SETS * G) + k + 1)
                    for j in range(GT):
                        ins = pe.transpose(ps[:, 6 + k % G % OB, P * j:P * (j + 1)], o_sb[:, k % OB, P * j:P * (j + 1)], ident[:])
                    ins.then_inc(o_turned, 1)

                turning = {min(s * (NB // SETS) + CHUNK_END[c] + LAG, NB - 1): s * G + c for s in range(SETS) for c in range(G)}
                scores(0)
                scores(1)
                for m in range(NB):
                    for n in (2 * m + 2, 2 * m + 3):
                        if n < NE:
                            scores(n)
                    values(m)
                    if m in turning:
                        turn_output(turning[m])
            pe.wait_ge(o_read, OB + NG * G)
            for g in range(G + 1):
                if g < G:
                    if g >= 2:
                        pe.wait_ge(copied, G * 3 + g - 1)
                    for k in range(GT):
                        ins = pe.transpose(ps[:, g % 2, P * k:P * (k + 1)], attn_tm[:, GT * g + k, :], ident[:])
                    ins.then_inc(turned, 1)
                if g >= 1:
                    pe.wait_ge(copied, G * 3 + g)
                    if g >= 3:
                        pe.wait_ge(x_new, G + g - 2)
                    by_tile(2 + (g - 1) % 2, g - 1, oT, wqo[:, 1, :], out_mm)
            feed_forward(1)


PREP_MM, PREP_DVE = 6, 5
CHUNK_END = [max(n for n, bank in enumerate(BANKS) if chunk_of(bank[0]) == c) // 4 for c in range(G)]


def bf16_bits(x):
    return (x.astype(np.float32).view(np.uint32) >> 16).astype(np.uint16)


def constants():
    inv = 1.0 / 10000.0 ** (np.arange(0, HD, 2, dtype=np.float32) / HD)
    ang = np.outer(np.arange(S, dtype=np.float32), inv)
    rope = np.stack([np.cos(ang), np.sin(ang)]).astype(np.float32)
    rope = np.tile(np.repeat(rope.transpose(0, 2, 1), 2, axis=1), (1, H, 1))
    te = np.arange(P)
    page = np.arange(S) // PAGE
    q_side = np.zeros((P - SHIFT_ROW, S))
    k_side = np.zeros((P - SHIFT_ROW, S))
    k_side[0:3] = 1
    rel = MASK_ROW - SHIFT_ROW
    q_side[rel:] = np.arange(PAGES)[:, None] > page[None, :]
    k_side[rel:] = np.where(np.arange(PAGES)[:, None] == page[None, :], MASKED, 0.0)
    return {
        "ident": np.eye(P, dtype=np.float32),
        "tri": bf16_bits(np.stack([np.triu(np.ones((P, P))), np.ones((P, P))], axis=1)),
        "tile_is": (te[:, None] // E == np.arange(T)[None, :]).astype(np.float32),
        "rank": np.tile(E - np.arange(E, dtype=np.float32), T),
        "e_is": np.ascontiguousarray(np.broadcast_to((np.arange(E)[:, None, None] == np.arange(E)[None, None, :]),
                                                     (E, T, E)).astype(np.float32)).reshape(-1),
        "head_of": bf16_bits(te[:, None] // HD == np.arange(H)[None, :]),
        "rope": rope,
        "template": bf16_bits(np.stack([q_side, k_side])),
    }


def kernel(**inputs):
    import concourse.bacc as _bacc
    from concourse.bass_utils import run_bass_kernel_spmd as _run

    v = {k: np.asarray(x) for k, x in inputs.items()}
    arrays = {
        "x": v["L0_attn_x"].reshape(S, D),
        "wv": v["L0_ffn_in_proj_w"][2 * D:3 * D], "bv": v["L0_ffn_in_proj_b"][2 * D:3 * D].reshape(D, 1),
        "woT": v["L0_ffn_out_proj_w"].T, "ob": v["L0_ffn_out_proj_b"],
        "g1c": np.stack([v["L0_ffn_ln1_g"], v["L0_ffn_ln1_b"]], axis=1),
        "lnb": np.stack([v["L0_ffn_ln1_g"], v["L0_ffn_ln1_b"], v["L0_ffn_ln2_g"], v["L0_ffn_ln2_b"]]),
        "wg": v["L0_ffn_wg"], "w1T": v["L0_ffn_w1"].transpose(0, 2, 1), "w2": v["L0_ffn_w2"],
        "b1_t": v["L0_ffn_b1"].reshape(E, P, FC).transpose(1, 2, 0), "b2_rep": np.tile(v["L0_ffn_b2"], (T, 1)),
        "wq": v["L0_attn_wq"], "wo": v["L0_attn_wo"], "w_downT": v["L0_attn_w_down"].T,
        "wk_up": v["L0_attn_wk_up"], "wv_up": v["L0_attn_wv_up"],
    }
    arrays.update(constants())
    arrays = {k: np.ascontiguousarray(x) for k, x in arrays.items()}
    nc = _bacc.Bacc("TRN2", target_bir_lowering=False, num_devices=1)
    a = {k: nc.dram_tensor(f"in_{k}", x.shape, mybir.dt.from_np(x.dtype), kind="ExternalInput").ap()
         for k, x in arrays.items()}
    out = nc.dram_tensor("out_rows", (S, D), F32, kind="ExternalOutput").ap()
    build(nc, a, out)
    r = _run(nc, [{f"in_{k}": x for k, x in arrays.items()}], core_ids=[0])
    return r.results[0]["out_rows"].reshape(1, S, D)
```

```python
from contextlib import ExitStack

import numpy as np
import concourse.bass as bass
from concourse import mybir
from concourse.alu_op_type import AluOpType as ALU

ACT = mybir.ActivationFunctionType
AX = mybir.AxisListType.X
F32 = mybir.dt.float32
BF16 = mybir.dt.bfloat16
I32 = mybir.dt.int32

P = 128
D = 128
S = 2048
T = S // P
G = 4
GT = T // G
GW = GT * P
E = 8
FF = 512
FC = FF // P
CAP = S // E
H = 16
HD = D // H
NG = 4
GH = H // NG
PAGE = 32
PAGES = S // PAGE
EPS = 1e-5
SCALE = float(HD) ** -0.5
SAFE = 40.0
MASKED = -1e30
Q_PIECE = (0, 0, 0, 1, 1, 2)
K_PIECE = (0, 1, 2, 0, 1, 0)
SHIFT_ROW = len(Q_PIECE) * HD
MASK_ROW = P - PAGES
VC = 32


def score_banks():
    banks = []
    for c in range(G):
        for j in range(GT * c):
            banks += [[(h, j, GW * c, GW, 0)] for h in range(GH)]
        j, q = GT * c, GW * c
        banks += [[(h, j, q, 4 * P, 0)] for h in range(GH)]
        banks += [[(h, j + 1, q + P, 3 * P, 0), (h, j + 3, q + 3 * P, P, 3 * P)] for h in range(GH)]
        banks += [[(h, j + 2, q + 2 * P, 2 * P, 0), (h + 1, j + 2, q + 2 * P, 2 * P, 2 * P)]
                  for h in range(0, GH, 2)]
    return banks


BANKS = score_banks()
SETS = 2
NE = SETS * len(BANKS) // 2
NB = SETS * len(BANKS) // 4
EB = 3
PB = 4
OB = 2
LAG = 2
assert len(BANKS) % 4 == 0 and NB % PB == 0


TE = GT * E
ORDER = (
    {
        "pe": "A0 W0 A1 P0 P1 D0 C0 D1 D2 L0 A2 C1 P2 R0 A3 D3 P3 K0 D4 L1 D5 D6 D7 R1 H0 K1 C2 C3 B0 E0 E1 L2 "
              "E2 E3 B1 R2 E4 E5 K2 E6 E7 L3 B2 E8 E9 R3 E10 E11 K3 E12 E13 B3 E14 T0 E15 T1 T2 T3",
        "act": "A0 A1 M0 M1 C0 L0 A2 C1 A3 D0 K0 M2 L1 M3 D1 K1 C2 C3 B0 E0 E1 E2 L2 E3 B1 E4 E5 K2 V0 E6 E7 L3 "
               "B2 S0 E8 E9 E10 E11 K3 E12 V1 E13 B3 E14 T0 E15 V2 S1 T1 S2 T2 S3 T3",
        "dve": "X0 X1 W0 X2 P0 P1 X3 L0 R0 P2 K0 P3 L1 R1 D0 K1 H0 E0 E1 L2 E2 R2 E3 K2 Z0 E4 E5 F0 L3 E6 E7 R3 "
               "E8 E9 K3 Z1 E10 E11 E12 F1 E13 Z2 E14 E15 F2 Z3 F3",
        "pool": "X0 X1 X2 P0 P1 X3 D0 B0 B1 B2 B3 P2 P3 E0 E1 E2 E3 Z0 E4 E5 F0 E6 E7 E8 E9 Z1 E10 E11 E12 E13 Z2 "
                "F1 E14 E15 F2 Z3 F3",
    },
    {
        "pe": "U0 U1 O0 U2 A0 U3 P0 O1 O2 A1 O3 P1 C0 L0 A2 E0 R0 E1 K0 C1 B0 L1 P2 A3 E2 E3 R1 P3 K1 E4 B1 C2 "
              "E5 L2 E6 E7 R2 C3 K2 E8 L3 B2 E9 R3 E10 E11 K3 E12 B3 E13 E14 E15",
        "act": "U0 U1 U2 A0 U3 A1 M0 C0 L0 A2 M1 E0 K0 C1 E1 B0 L1 A3 E2 E3 M2 K1 E4 B1 C2 E5 M3 L2 E6 E7 V0 K2 "
               "C3 E8 L3 B2 E9 E10 V1 E11 K3 E12 B3 E13 E14 E15 V2",
        "dve": "O0 X0 P0 O1 X1 O2 O3 P1 L0 X2 R0 X3 K0 E0 L1 E1 P2 R1 E2 K1 E3 P3 E4 Z0 L2 E5 R2 E6 K2 E7 F0 L3 "
               "E8 R3 Z1 E9 K3 E10 F1 E11 E12 Z2 E13 E14 E15 F2 Z3 F3",
        "pool": "B0 X0 P0 X1 B1 B2 P1 X2 X3 B3 E0 E1 P2 E2 E3 P3 E4 Z0 E5 E6 E7 E8 Z1 E9 E10 E11 E12 Z2 E13 E14 "
                "E15 Z3",
    },
)


def steps(n, engine):
    return [(word[0], int(word[1:])) for word in ORDER[n][engine].split()]


def chunk_of(block):
    return block[2] // GW


def previous_exp(n):
    return n - EB if n >= EB else max(m for m in range(NE) if m % EB == n % EB) - NE


def build(nc, a, out):
    with ExitStack() as ctx:
        def sb(name, shape, dt=F32):
            return ctx.enter_context(nc.sbuf_tensor(name, shape, dt))

        def sem(name):
            return ctx.enter_context(nc.semaphore(name))

        ps = ctx.enter_context(nc.psum_tensor("ps", [P, 8, 512], F32))

        ident = sb("ident", [P, P])
        tri_bf = sb("tri_bf", [P, 2, P], BF16)
        tile_is = sb("tile_is", [TE, GT])
        rank = sb("rank", [P, T, E])
        neg_half = sb("neg_half", [P, GT])
        w_mha = sb("w_mha", [P, D])
        b_mha = sb("b_mha", [P, D])
        centre = sb("centre", [P, D])
        g1c = sb("g1c", [P, 2])
        lnb = sb("lnb", [P, 2, D])
        wg = sb("wg", [P, E])
        w12 = sb("w12", [P, E * D])
        b12_big = sb("b12_big", [TE, GT, D])
        wqo = sb("wqo", [P, 2, D])
        wdu = sb("wdu", [64, 3, D])
        wkv = sb("wkv", [P, 2, D])
        wsw = sb("wsw", [P, 2, D])
        x_tm = sb("x_tm", [P, T, D])
        trio = sb("trio", [P, 3 * S])
        xT = trio[:, 0:S]
        sin = trio[:, S:2 * S]
        cos = trio[:, 2 * S:3 * S]
        attn_tm = trio[:, 2 * S:3 * S].rearrange("p (t d) -> p t d", d=D)
        stats = sb("stats", [P, T, 6])
        mv = sb("mv", [P, T, 2])
        var_eps = sb("var_eps", [P, T])
        rstd = sb("rstd", [P, T])
        neg_mean = sb("neg_mean", [P, T])
        offset = sb("offset", [P, T])
        row_max = sb("row_max", [P, T])
        row_sum = sb("row_sum", [P, T])
        row_pick = sb("row_pick", [P, T])
        gate = sb("gate", [P, T])
        pick_bf = sb("pick_bf", [P, T * E], BF16)
        pick = sb("pick", [P, T, E])
        coefT = sb("coefT", [TE, G, P])
        arena = sb("arena", [P, 14336])

        def rows(k):
            return arena[:, S * k:S * (k + 1)].rearrange("p (t d) -> p t d", d=D)

        xn, y, base, xb, y1T = rows(0), rows(1), rows(2), rows(3), arena[:, 4 * S:5 * S]
        prod = arena[:, 10240:11264].rearrange("p (b n) -> p b n", b=2)
        pair = arena[:, 12288:13312].rearrange("p (b n) -> p b n", b=2)
        quad = arena[:, 13312:13824].rearrange("p (b n) -> p b n", b=2)
        logit = arena[:, 13824:13952].rearrange("p (t e) -> p t e", e=E)
        expo = arena[:, 13952:14080].rearrange("p (t e) -> p t e", e=E)
        coef = arena[:, 14080:14208].rearrange("p (t e) -> p t e", e=E)
        ranked = arena[:, 14208:14336].rearrange("p (t e) -> p t e", e=E)
        piece = arena[:, 0:6144].bitcast(BF16).rearrange("p (s k n) -> p s k n", s=2, k=3)
        pexp = arena[:, 6144:14336].rearrange("p (b n) -> p b n", b=2 * PB)
        rope = arena[:, 6144:10240].rearrange("p (b k n) -> p b k n", b=2, k=4)
        square = arena[:, 10240:12288].bitcast(BF16).rearrange("p (w n) -> p w n", w=2 * G)
        shift = arena[0:H, 9216:11264]
        shift_rest = arena[0:H, 11264:13312]
        shift3 = arena[0:H, 6144:9216].bitcast(BF16).rearrange("h (k n) -> h k n", k=3)
        oT = arena[:, 12288:14336]
        packed = sb("packed", [P, SETS, 2, GH, S], BF16)
        fold = packed[:].rearrange("p a b h n -> p (a b h n)").bitcast(F32)
        w1T = fold[:, 0:4096].rearrange("p (e c d) -> p e c d", e=E, c=FC)
        w2 = fold[:, 4096:8192].rearrange("p (e c d) -> p e c d", e=E, c=FC)
        b1_t = fold[:, 12288:12320].rearrange("p (c e) -> p c e", c=FC)
        b12_cols = fold[:, 12320:12320 + TE].rearrange("p (t e) -> p t e", e=E)
        b2_t = fold[:, 13440:13440 + E]
        wv = fold[:, 13568:13696]
        woT = fold[:, 13696:13824]
        bv = fold[:, 13824:13825]
        bv_rep = fold[:, 13952:14080]
        ob_rep = fold[:, 14080:14208]
        v_tm = sb("v_tm", [P, T, D])
        v_st = sb("v_st", [P, SETS, T, GH, VC])
        o_sb = sb("o_sb", [P, 2, GW])
        den = sb("den", [P, 2, GT, GH])
        head_of = sb("head_of", [P, H], BF16)
        half = sb("half", [H, 2])
        longest = sb("longest", [H, 2])
        ratio = sb("ratio", [H, 4])
        line = sb("line", [H, 2])
        beyond = sb("beyond", [H, 2])
        flag = sb("flag", [1, 1], I32)
        top = sb("top", [P, P])
        topT = sb("topT", [GH * T, P])
        piece_dram = nc.dram_tensor("piece_dram", [2, 3, H, HD, S], BF16).ap()
        shift_dram = nc.dram_tensor("shift_dram", [H, S], F32).ap()
        shift3_dram = nc.dram_tensor("shift3_dram", [3, H, S], BF16).ap()

        x_in = [sem(f"x_in{g}") for g in range(G)]
        w_in = [sem(f"w_in{e}") for e in range(E)]
        packed_in = [sem(f"packed_in{s}") for s in range(SETS)]
        const_in, mha_in, route_in, fold_in, att_in, rope_in, template_in = (sem(n) for n in
            ("const_in", "mha_in", "route_in", "fold_in", "att_in", "rope_in", "template_in"))
        prep_pool, prep_dve, prep_act, prep_mm = (sem(n) for n in ("prep_pool", "prep_dve", "prep_act", "prep_mm"))
        ln_part, ln_stats, ln_var, ln_rstd, ln_offset, normed = ([sem(f"{n}_{kind}") for kind in ("rows", "ln1", "ln2", "attn")]
            for n in ("ln_part", "ln_stats", "ln_var", "ln_rstd", "ln_offset", "normed"))
        turned, copied = ([sem(f"{n}_{kind}") for kind in ("rows", "y1", "out", "attn")] for n in ("turned", "copied"))
        mha_mm, mha_read, logit_mm = sem("mha_mm"), sem("mha_read"), sem("logit_mm")
        max_ready, kept, high_mm, low_mm = (sem(n) for n in ("max_ready", "kept", "high_mm", "low_mm"))
        route, logit_sub, exp_ready, pick_ready, place_mm, coef_ready, coef_mm, coefT_ready = (sem(n) for n in
            ("route", "logit_sub", "exp_ready", "pick_ready", "place_mm", "coef_ready", "coef_mm", "coefT_ready"))
        xb_ready, bias_mm, bias_read = (sem(n) for n in ("xb_ready", "bias_mm", "bias_read"))
        high_ready, pair_ready, quad_ready, z_ready = (sem(n) for n in
            ("high_ready", "pair_ready", "quad_ready", "z_ready"))
        z_part, x_new = sem("z_part"), sem("x_new")
        proj_mm, rope_part, rotated, high_piece, rest_ready, mid_piece, low_piece = (sem(n) for n in
            ("proj_mm", "rope_part", "rotated", "high_piece", "rest_ready", "mid_piece", "low_piece"))
        v_mm, v_ready, v_staged, piece_out = (sem(n) for n in ("v_mm", "v_ready", "v_staged", "piece_out"))
        max_in, max_mm, max_read, top_mm, top_ready, top_out = (sem(n) for n in
            ("max_in", "max_mm", "max_read", "top_mm", "top_ready", "top_out"))
        squared, norm_mm, bound, root_ready, beyond_mm, flag_ready, true_shift = (sem(n) for n in
            ("squared", "norm_mm", "bound", "root_ready", "beyond_mm", "flag_ready", "true_shift"))
        shift_in, shift_ready, shift_out = (sem(n) for n in ("shift_in", "shift_ready", "shift_out"))
        score_mm, exp_done, pv_done = sem("score_mm"), sem("exp_done"), sem("pv_done")
        o_copied, o_turned, den_ready, o_read = (sem(n) for n in ("o_copied", "o_turned", "den_ready", "o_read"))
        out_mm, stored = sem("out_mm"), sem("stored")

        block = ctx.enter_context(nc.Block())

        ROWS, LN1, LN2, ATTN = range(4)
        Y1, OUT = 1, 2
        CHAIN, BIAS, MISC = 4, 6, 7

        def cols(g):
            return slice(GW * g, GW * (g + 1))

        def bank_tiles(b):
            return ps[:, b, :].rearrange("p (t d) -> p t d", d=D)

        def rows_of(v, n=GT):
            return v.unsqueeze(1).to_broadcast([P, n, D])

        def group(g):
            return slice(GT * g, GT * (g + 1))

        def normed_groups(kind):
            return {ROWS: 0, LN2: G - 1}.get(kind, G)

        SMALL, MHA, ROUTE, FOLD = 3, 6, 4, 2
        PACK_DMAS = len(Q_PIECE) + len(K_PIECE)

        @block.sync
        def _(sp):
            def load_x(g):
                sp.dma_start(x_tm[:, group(g), :],
                             a["x"][cols(g), :].rearrange("(t p) d -> p t d", p=P)).then_inc(x_in[g], 16)

            load_x(0)
            for dst, src in ((ident[:], a["ident"]), (centre[:], a["centre"]), (wv, a["wv"]), (woT, a["woT"]), (bv, a["bv"]),
                             (ob_rep, a["ob"].partition_broadcast(P))):
                sp.dma_start(dst, src).then_inc(mha_in, 16)
            for g in range(1, G):
                load_x(g)
            for dst, src in ((g1c[:], a["g1c"]), (wg[:], a["wg"]), (tri_bf[:], a["tri"].bitcast(BF16)),
                             (rank[:], a["rank"].partition_broadcast(P))):
                sp.dma_start(dst, src).then_inc(route_in, 16)
            sp.dma_start(b1_t, a["b1_t"]).then_inc(fold_in, 16)
            sp.dma_start(b2_t, a["b2_t"]).then_inc(fold_in, 16)
            for dst, src in ((lnb[:], a["lnb"].partition_broadcast(P)), (tile_is[:], a["tile_is"]),
                             (head_of[:], a["head_of"].bitcast(BF16))):
                sp.dma_start(dst, src).then_inc(const_in, 16)
            for e in range(E):
                sp.dma_start(w1T[:, e, :, :], a["w1T"][e].rearrange("(p c) d -> p c d", c=FC)).then_inc(w_in[e], 16)
                sp.dma_start(w2[:, e, :, :], a["w2"][e].rearrange("(p c) d -> p c d", c=FC)).then_inc(w_in[e], 16)
            for dst, src in ((wqo[:, 0, :], a["wq"]), (wqo[:, 1, :], a["wo"]), (wdu[:, 0, :], a["w_downT"]),
                             (wdu[:, 1, :], a["wk_up"]), (wdu[:, 2, :], a["wv_up"])):
                sp.dma_start(dst, src).then_inc(att_in, 16)
            for i, dst in enumerate((cos, sin)):
                sp.dma_start(dst, a["rope"][i]).then_inc(rope_in, 16)
            sp.wait_ge(prep_mm, PREP_MM)
            sp.wait_ge(prep_dve, PREP_DVE)
            for s in range(SETS):
                for side in range(2):
                    src = a["template"][side].bitcast(BF16).unsqueeze(1).to_broadcast([P - SHIFT_ROW, GH, S])
                    sp.dma_start(packed[SHIFT_ROW:P, s, side, :, :], src).then_inc(template_in, 16)
            for g in range(G):
                for side in range(2):
                    sp.wait_ge(low_piece, 2 * g + side + 1)
                    dst = piece_dram[side, :, :, :, cols(g)].rearrange("k h d n -> (h d) k n")
                    sp.dma_start(dst, piece[:, side, :, cols(g)]).then_inc(piece_out, 16)
            sp.wait_ge(piece_out, 16 * 2 * G)
            sp.wait_ge(template_in, 16 * SETS * 2)

            def load_packed(s, first_head, done):
                for side, pieces in enumerate((Q_PIECE, K_PIECE)):
                    for b, k in enumerate(pieces):
                        src = piece_dram[side, k, bass.ds(first_head, GH), :, :].rearrange("h d n -> d h n")
                        sp.dma_start(packed[HD * b:HD * (b + 1), s, side, :, :], src).then_inc(done, 16)

            load_packed(0, 0, packed_in[0])
            sp.wait_ge(flag_ready, 1)
            beyond_safe = sp.value_load(flag[0:1, 0:1], min_val=0, max_val=H)
            with sp.If(beyond_safe > 0):
                sp.wait_ge(packed_in[0], 16 * PACK_DMAS)
                sp.sem_inc(top_out, 16)
                with sp.Fori(0, NG) as g:
                    sp.wait_ge(top_mm, g + 1)
                    load_packed(0, g * GH, max_in)
                    sp.wait_ge(top_ready, g + 2)
                    dst = shift_dram[bass.ds(g * GH, GH), :].rearrange("h (t p) -> (h t) p", p=P)
                    sp.dma_start(dst, topT[:, :]).then_inc(top_out, 16)
                sp.wait_ge(top_out, 16 + 16 * NG)
                sp.dma_start(shift, shift_dram[:, :]).then_inc(shift_in, 16)
                sp.wait_ge(top_mm, 1 + NG)
                load_packed(0, 0, max_in)
                sp.wait_ge(max_in, 16 * PACK_DMAS * (NG + 1))
            sp.wait_ge(shift_ready, 1)
            sp.dma_start(shift3_dram.rearrange("k h n -> h k n"), shift3).then_inc(shift_out, 16)
            sp.wait_ge(shift_out, 16)
            for g in range(NG):
                if g >= SETS:
                    sp.wait_ge(score_mm, (g - SETS + 1) * NE // SETS)
                if g >= 1:
                    load_packed(g % SETS, g * GH, packed_in[g % SETS])
                sp.dma_start(packed[SHIFT_ROW:SHIFT_ROW + 3, g % SETS, 0, :, :],
                             shift3_dram[:, GH * g:GH * (g + 1), :]).then_inc(packed_in[g % SETS], 16)
            for g in range(G):
                sp.wait_ge(x_new, 2 * G + g + 1)
                sp.dma_start(out[cols(g), :].rearrange("(t p) d -> p t d", p=P),
                             x_tm[:, GT * g:GT * (g + 1), :]).then_inc(stored, 16)
            sp.wait_ge(stored, 16 * G)

        @block.gpsimd
        def _(pool):
            def ln_rsqrt(kind, n, g):
                t, q, with_offset = group(g), G * n + g, g < normed_groups(kind)
                pool.wait_ge(ln_stats[kind], q + 1)
                pool.tensor_scalar(var_eps[:, t], mv[:, t, 1], EPS, None, ALU.add).then_inc(ln_var[kind], 1)
                if with_offset:
                    pool.tensor_scalar(neg_mean[:, t], mv[:, t, 0], -1.0, None, ALU.mult).then_inc(ln_offset[kind], 1)
                pool.wait_ge(ln_var[kind], q + 1)
                pool.tensor_tensor(rstd[:, t], var_eps[:, t], neg_half[:], ALU.pow).then_inc(ln_rstd[kind], 1)
                if with_offset:
                    pool.wait_ge(ln_rstd[kind], q + 1)
                    pool.wait_ge(ln_offset[kind], 2 * (normed_groups(kind) * n + g) + 1)
                    pool.tensor_tensor(offset[:, t], neg_mean[:, t], rstd[:, t], ALU.mult).then_inc(ln_offset[kind], 1)

            pool.memset(neg_half[:], -0.5).then_inc(prep_pool, 1)
            pool.wait_ge(prep_pool, 1)

            def feed_forward(n):
                for step, g in steps(n, "pool"):
                    if step == "X":
                        ln_rsqrt(ROWS, n, g)
                    elif step == "P":
                        ln_rsqrt(LN1, n, g)
                    elif step == "Z":
                        ln_rsqrt(LN2, n, g)
                    elif step == "F" and n == 0:
                        ln_rsqrt(ATTN, n, g)
                    elif step == "D":
                        pool.wait_ge(const_in, 16 * SMALL)
                        pool.tensor_scalar(lnb[:], lnb[:], 0.5, None, ALU.mult).then_inc(prep_pool, 1)
                        pool.wait_ge(prep_pool, 2)
                    elif step == "B":
                        pool.wait_ge(x_new if n else x_in[g], G + g + 1 if n else 16)
                        pool.tensor_tensor(xb[:, group(g), :], x_tm[:, group(g), :], rows_of(lnb[:, 1, :]),
                                           ALU.add).then_inc(xb_ready, 1)
                    elif step == "E":
                        t, k = g, T * n + g
                        pool.wait_ge(pair_ready, k + 1)
                        if t >= 2:
                            pool.wait_ge(z_ready, k - 1)
                        q = quad[:, t % 2, :]
                        pool.tensor_tensor(q, pair[:, t % 2, 0:2 * D], pair[:, t % 2, 2 * D:4 * D],
                                           ALU.add).then_inc(quad_ready, 1)
                        pool.wait_ge(quad_ready, 2 * k + 1)
                        pool.tensor_tensor(q[:, 0:D], q[:, 0:D], q[:, D:2 * D], ALU.add).then_inc(quad_ready, 1)
                        pool.wait_ge(quad_ready, 2 * k + 2)
                        if t % GT == 0:
                            pool.wait_ge(bias_read, G * n + t // GT + 1)
                        pool.tensor_tensor(y[:, t, :], q[:, 0:D], base[:, t, :], ALU.add).then_inc(z_ready, 1)

            feed_forward(0)
            pool.memset(v_st[:], 1.0).then_inc(v_staged, 1)
            pool.memset(half[:, 0:1], 0.5).then_inc(root_ready, 1)
            pool.memset(half[:, 1:2], -0.5).then_inc(root_ready, 1)
            for w in range(2 * G):
                pool.wait_ge(rope_part, 2 * w + 2)
                if w >= 2:
                    pool.wait_ge(rest_ready, w - 1)
                    pool.wait_ge(squared, w - 1)
                pool.tensor_tensor(rope[:, w % 2, 2, :], rope[:, w % 2, 0, :], rope[:, w % 2, 1, :],
                                   ALU.add).then_inc(rotated, 1)
            pool.wait_ge(root_ready, 2)
            pool.wait_ge(bound, 6)
            pool.tensor_tensor(ratio[:, 2:4], ratio[:, 1:2].to_broadcast([H, 2]), half[:], ALU.pow).then_inc(root_ready, 1)
            pool.wait_ge(v_ready, G)
            pool.wait_ge(v_staged, 1)
            for g in range(NG):
                if g >= SETS:
                    pool.wait_ge(pv_done, PB + (g - SETS + 1) * NB // SETS)
                pool.tensor_copy(v_st[:, g % SETS, :, :, 0:HD],
                                 v_tm[:, :, GH * HD * g:GH * HD * (g + 1)].rearrange("p t (h d) -> p t h d", d=HD)
                                 ).then_inc(v_staged, 1)
            feed_forward(1)

        @block.scalar
        def _(act):
            def normalise(kind, n, g, src, dst):
                act.wait_ge(ln_offset[kind], 2 * (normed_groups(kind) * n + g) + 2)
                for t in range(GT * g, GT * (g + 1)):
                    ins = nc.scalar.activation(dst[:, t, :], src[:, t, :], ACT.Identity,
                                               bias=offset[:, t:t + 1], scale=rstd[:, t:t + 1])
                ins.then_inc(normed[kind], 1)

            def copy_turned(kind, n, g, bank, dst):
                act.wait_ge(turned[kind], G * n + g + 1)
                nc.scalar.activation(dst[:, cols(g)], ps[:, bank, :], ACT.Copy).then_inc(copied[kind], 1)

            def feed_forward(n):
                for step, g in steps(n, "act"):
                    q, bank = G * n + g, CHAIN + g % 2
                    if step == "U":
                        copy_turned(OUT, 0, g, g % 2, oT)
                    elif step == "A":
                        copy_turned(ROWS, n, g, bank, xT)
                    elif step == "M":
                        normalise(LN1, n, g, y, y)
                    elif step == "C":
                        act.wait_ge(route_in, 16 * ROUTE)
                        act.wait_ge(turned[Y1], q + 1)
                        nc.scalar.activation(y1T[:, cols(g)], ps[:, bank, :], ACT.Identity,
                                             bias=g1c[:, 1:2], scale=g1c[:, 0:1]).then_inc(copied[Y1], 1)
                    elif step == "L":
                        act.wait_ge(logit_sub, q + 1)
                        nc.scalar.activation(expo[:, group(g), :], logit[:, group(g), :], ACT.Exp).then_inc(exp_ready, 1)
                    elif step == "D":
                        act.wait_ge(prep_mm, 4 + g)
                        nc.scalar.activation(w12[:, 512 * g:512 * (g + 1)], ps[:, g, :], ACT.Copy).then_inc(prep_act, 1)
                    elif step == "K":
                        act.wait_ge(coef_mm, q + 1)
                        nc.scalar.activation(coefT[:, g, :], ps[0:TE, MISC, P * (2 + g % 2):P * (3 + g % 2)],
                                             ACT.Copy).then_inc(coefT_ready, 1)
                    elif step == "B":
                        act.wait_ge(bias_mm, q + 1)
                        nc.scalar.activation(base[:, group(g), :], bank_tiles(BIAS), ACT.Copy).then_inc(bias_read, 1)
                    elif step == "E":
                        t, k = g, T * n + g
                        act.wait_ge(high_mm, k + 1)
                        act.wait_ge(coef_ready, G * n + t // GT + 1)
                        if t >= 2:
                            act.wait_ge(pair_ready, k - 1)
                        for e in range(E // 2, E):
                            cut = slice(D * (e - E // 2), D * (e - E // 2 + 1))
                            ins = nc.scalar.activation(prod[:, t % 2, cut], ps[:, t % 2, cut], ACT.Copy,
                                                       scale=coef[:, t, e:e + 1])
                        ins.then_inc(high_ready, 1)
                    elif step == "V":
                        normalise(LN2, n, g, y, y)
                    elif step == "S":
                        normalise(ATTN, n, g, x_tm, xn)
                    elif step == "T":
                        copy_turned(ATTN, n, g, bank, xT)

            feed_forward(0)
            for w in range(2 * G + 1):
                if w < 2 * G:
                    act.wait_ge(rotated, w + 1)
                    nc.scalar.activation(piece[:, w % 2, 0, cols(w // 2)], rope[:, w % 2, 2, :],
                                         ACT.Copy).then_inc(high_piece, 1)
                    nc.scalar.activation(square[:, w, :], rope[:, w % 2, 2, :], ACT.Square).then_inc(squared, 1)
                if w >= 1:
                    act.wait_ge(rest_ready, w)
                    nc.scalar.activation(piece[:, (w - 1) % 2, 1, cols((w - 1) // 2)], rope[:, (w - 1) % 2, 3, :],
                                         ACT.Copy).then_inc(mid_piece, 1)
            for g in range(G):
                act.wait_ge(v_mm, g + 1)
                nc.scalar.activation(v_tm[:, GT * g:GT * (g + 1), :], bank_tiles(g), ACT.Copy).then_inc(v_ready, 1)
            act.sem_inc(exp_done, EB)
            with act.Fori(0, NG // SETS) as i:
                for n in range(NE):
                    act.wait_ge(score_mm, i * NE + n + 1)
                    if n % 2 == 0:
                        act.wait_ge(pv_done, i * NB + n // 2 + 1)
                    src = ps[:, 2 * (n % EB):2 * (n % EB) + 2, :].rearrange("p b n -> p (b n)")
                    nc.scalar.activation(pexp[:, 2 * (n // 2 % PB) + n % 2, :], src, ACT.Exp,
                                         scale=SCALE).then_inc(exp_done, 1)
            feed_forward(1)

        @block.vector
        def _(dve):
            def ln_stats_of(kind, n, g, src):
                for t in range(GT * g, GT * (g + 1)):
                    ins = dve.bn_stats(stats[:, t, :], src[:, t, :])
                ins.then_inc(ln_part[kind], 1)
                dve.wait_ge(ln_part[kind], G * n + g + 1)
                for t in range(GT * g, GT * (g + 1)):
                    ins = dve.bn_aggr(mv[:, t, :], stats[:, t, :])
                ins.then_inc(ln_stats[kind], 1)

            def by_expert(bank_cols, g):
                return ps[:, MISC, bank_cols + TE * g:bank_cols + TE * (g + 1)].rearrange("p (t e) -> p t e", e=E)

            def over_experts(v, g):
                return v[:, group(g)].unsqueeze(2).to_broadcast([P, GT, E])

            def feed_forward(n):
                for step, g in steps(n, "dve"):
                    q, tt = G * n + g, group(g)
                    if step == "O":
                        dve.wait_ge(out_mm, g + 1)
                        dve.tensor_tensor(x_tm[:, tt, :], x_tm[:, tt, :], bank_tiles(2 + g % 2), ALU.add).then_inc(x_new, 1)
                    elif step == "X":
                        dve.wait_ge(x_new if n else x_in[g], G + g + 1 if n else 16)
                        ln_stats_of(ROWS, n, g, x_tm)
                    elif step == "W":
                        dve.wait_ge(mha_in, 16 * MHA)
                        dve.tensor_copy(bv_rep, bv.to_broadcast([P, D])).then_inc(prep_dve, 1)
                        dve.wait_ge(prep_mm, 2)
                        dve.tensor_tensor(w_mha[:], ps[:, BIAS, 0:D], ident[:], ALU.add).then_inc(prep_dve, 1)
                        dve.tensor_tensor(b_mha[:], ps[:, BIAS, D:2 * D], ob_rep, ALU.add).then_inc(prep_dve, 1)
                        dve.wait_ge(prep_mm, 3)
                        dve.tensor_copy(w_mha[:], ps[:, BIAS, 2 * D:3 * D]).then_inc(prep_dve, 1)
                    elif step == "P":
                        dve.wait_ge(mha_mm, q + 1)
                        dve.wait_ge(ln_rstd[ROWS], q + 1)
                        if n == 0:
                            dve.wait_ge(prep_dve, 3)
                        for t in range(GT * g, GT * (g + 1)):
                            ins = dve.scalar_tensor_tensor(y[:, t, :], ps[:, CHAIN + g % 2, D * (t % GT):D * (t % GT + 1)],
                                                           rstd[:, t:t + 1], b_mha[:], ALU.mult, ALU.add)
                        ins.then_inc(mha_read, 1)
                        dve.wait_ge(mha_read, q + 1)
                        ln_stats_of(LN1, n, g, y)
                    elif step == "L":
                        dve.wait_ge(logit_mm, q + 1)
                        dve.tensor_reduce(row_max[:, tt], by_expert(0, g), AX, ALU.max).then_inc(max_ready, 1)
                        dve.wait_ge(max_ready, q + 1)
                        dve.tensor_tensor(logit[:, tt, :], by_expert(0, g), over_experts(row_max, g),
                                          ALU.subtract).then_inc(logit_sub, 1)
                    elif step == "R":
                        if n == 0:
                            dve.wait_ge(route_in, 16 * ROUTE)
                        dve.wait_ge(exp_ready, q + 1)
                        dve.tensor_reduce(row_sum[:, tt], expo[:, tt, :], AX, ALU.add).then_inc(route, 1)
                        dve.scalar_tensor_tensor(ranked[:, tt, :], expo[:, tt, :], 1.0, rank[:, tt, :],
                                                 ALU.is_ge, ALU.mult).then_inc(route, 1)
                        dve.wait_ge(route, 4 * q + 2)
                        dve.tensor_reduce(row_pick[:, tt], ranked[:, tt, :], AX, ALU.max).then_inc(route, 1)
                        dve.reciprocal(gate[:, tt], row_sum[:, tt]).then_inc(route, 1)
                        dve.wait_ge(route, 4 * q + 4)
                        dve.tensor_tensor(pick_bf[:, TE * g:TE * (g + 1)].rearrange("p (t e) -> p t e", e=E), ranked[:, tt, :],
                                          over_experts(row_pick, g), ALU.is_equal).then_inc(pick_ready, 1)
                        dve.tensor_tensor(pick[:, tt, :], ranked[:, tt, :], over_experts(row_pick, g),
                                          ALU.is_equal).then_inc(pick_ready, 1)
                    elif step == "K":
                        dve.wait_ge(place_mm, q + 1)
                        dve.wait_ge(pick_ready, 2 * q + 2)
                        dve.scalar_tensor_tensor(pick[:, tt, :], by_expert(P, g), float(CAP), pick[:, tt, :],
                                                 ALU.is_le, ALU.mult).then_inc(kept, 1)
                        dve.wait_ge(kept, q + 1)
                        dve.tensor_tensor(coef[:, tt, :], pick[:, tt, :], over_experts(gate, g), ALU.mult).then_inc(coef_ready, 1)
                        dve.wait_ge(coef_ready, q + 1)
                    elif step == "D":
                        dve.wait_ge(fold_in, 16 * FOLD)
                        dve.wait_ge(prep_mm, 6)
                        dve.tensor_tensor(b12_cols, ps[:, 2, 0:E].unsqueeze(1).to_broadcast([P, GT, E]),
                                          b2_t.unsqueeze(1).to_broadcast([P, GT, E]), ALU.add).then_inc(prep_dve, 1)
                    elif step == "H":
                        dve.wait_ge(prep_mm, 7)
                        dve.wait_ge(const_in, 16 * SMALL)
                        dve.tensor_tensor(b12_big[:], ps[0:TE, 2, P:2 * P].unsqueeze(1).to_broadcast([TE, GT, D]),
                                          tile_is[:].unsqueeze(2).to_broadcast([TE, GT, D]), ALU.mult).then_inc(prep_dve, 1)
                        dve.wait_ge(prep_mm, 8)
                        dve.tensor_copy(wkv[:].rearrange("p a d -> p (a d)"), ps[:, 3, 0:2 * D]).then_inc(prep_dve, 1)
                    elif step == "E":
                        t, k = g, T * n + g
                        dve.wait_ge(low_mm, k + 1)
                        dve.wait_ge(high_ready, k + 1)
                        if t >= 2:
                            dve.wait_ge(quad_ready, 2 * (k - 2) + 1)
                        for e in range(E // 2):
                            ins = dve.scalar_tensor_tensor(pair[:, t % 2, D * e:D * (e + 1)],
                                                           ps[:, 2 + t % 2, D * e:D * (e + 1)], coef[:, t, e:e + 1],
                                                           prod[:, t % 2, D * e:D * (e + 1)], ALU.mult, ALU.add)
                        ins.then_inc(pair_ready, 1)
                    elif step == "Z":
                        dve.wait_ge(z_ready, T * n + GT * (g + 1))
                        ln_stats_of(LN2, n, g, y)
                    elif step == "F":
                        if g < G - 1:
                            dve.wait_ge(normed[LN2], (G - 1) * n + g + 1)
                            dve.tensor_tensor(y[:, tt, :], y[:, tt, :], rows_of(lnb[:, 0, :]), ALU.mult).then_inc(z_part, 1)
                            dve.wait_ge(z_part, q + 1)
                            dve.wait_ge(xb_ready, q + 1)
                            dve.tensor_tensor(x_tm[:, tt, :], y[:, tt, :], xb[:, tt, :], ALU.add).then_inc(x_new, 1)
                        else:
                            dve.wait_ge(ln_stats[LN2], q + 1)
                            for t in range(GT * g, GT * (g + 1)):
                                ins = dve.scalar_tensor_tensor(y[:, t, :], y[:, t, :], mv[:, t, 0:1], lnb[:, 0, :],
                                                               ALU.subtract, ALU.mult)
                            ins.then_inc(z_part, 1)
                            dve.wait_ge(z_part, q + 1)
                            dve.wait_ge(ln_rstd[LN2], q + 1)
                            dve.wait_ge(xb_ready, q + 1)
                            for t in range(GT * g, GT * (g + 1)):
                                ins = dve.scalar_tensor_tensor(x_tm[:, t, :], y[:, t, :], rstd[:, t:t + 1], xb[:, t, :],
                                                               ALU.mult, ALU.add)
                            ins.then_inc(x_new, 1)
                        if n == 0:
                            dve.wait_ge(x_new, g + 1)
                            ln_stats_of(ATTN, n, g, x_tm)

            feed_forward(0)

            dve.wait_ge(att_in, 16 * 5)
            for k, w in enumerate((wqo[:, 0, :], wkv[:, 0, :])):
                even_odd = w.rearrange("p (n two) -> p n two", two=2)
                to = wsw[:, k, :].rearrange("p (n two) -> p n two", two=2)
                dve.tensor_scalar(to[:, :, 0], even_odd[:, :, 1], -1.0, None, ALU.mult).then_inc(prep_dve, 1)
                dve.tensor_copy(to[:, :, 1], even_odd[:, :, 0]).then_inc(prep_dve, 1)
            dve.wait_ge(rope_in, 16 * 2)
            for w in range(2 * G + 2):
                if w < 2 * G:
                    g, side = w // 2, w % 2
                    dve.wait_ge(proj_mm, w + 1)
                    if w >= 2:
                        dve.wait_ge(rotated, w - 1)
                    for k, table in enumerate((cos, sin)):
                        dve.tensor_tensor(rope[:, w % 2, k, :], ps[:, 4 * (g % 2) + 2 * side + k, :],
                                          table[:, cols(g)], ALU.mult).then_inc(rope_part, 1)
                if 1 <= w <= 2 * G:
                    v = w - 1
                    dve.wait_ge(high_piece, v + 1)
                    if v >= 2:
                        dve.wait_ge(low_piece, v - 1)
                    dve.tensor_tensor(rope[:, v % 2, 3, :], rope[:, v % 2, 2, :], piece[:, v % 2, 0, cols(v // 2)],
                                      ALU.subtract).then_inc(rest_ready, 1)
                if w >= 2:
                    v = w - 2
                    dve.wait_ge(mid_piece, v + 1)
                    dve.tensor_tensor(piece[:, v % 2, 2, cols(v // 2)], rope[:, v % 2, 3, :],
                                      piece[:, v % 2, 1, cols(v // 2)], ALU.subtract).then_inc(low_piece, 1)

            norms = [ps[0:H, 4 * b:4 * b + 4, :].rearrange("h b n -> h (b n)") for b in (1, 0)]
            for side in range(2):
                dve.wait_ge(norm_mm, side + 1)
                dve.tensor_reduce(longest[:, side:side + 1], norms[side], AX, ALU.max).then_inc(bound, 1)
            dve.wait_ge(bound, 2)
            dve.tensor_scalar(longest[:], longest[:], 1e-12, None, ALU.max).then_inc(bound, 1)
            dve.wait_ge(bound, 3)
            dve.reciprocal(ratio[:, 0:1], longest[:, 0:1]).then_inc(bound, 1)
            dve.tensor_tensor(beyond[:, 0:1], longest[:, 0:1], longest[:, 1:2], ALU.mult).then_inc(bound, 1)
            dve.wait_ge(bound, 5)
            dve.tensor_tensor(ratio[:, 1:2], ratio[:, 0:1], longest[:, 1:2], ALU.mult).then_inc(bound, 1)
            dve.tensor_scalar(beyond[:, 1:2], beyond[:, 0:1], (SAFE / SCALE) ** 2, None, ALU.is_le).then_inc(bound, 1)
            dve.memset(shift3[:, 1:3, :], 0.0).then_inc(bound, 1)
            dve.wait_ge(root_ready, 3)
            dve.tensor_scalar(line[:, 0:1], ratio[:, 2:3], -0.51, None, ALU.mult).then_inc(bound, 1)
            dve.tensor_scalar(line[:, 1:2], longest[:, 1:2], ratio[:, 3:4], -0.51, ALU.mult, ALU.mult).then_inc(bound, 1)
            dve.wait_ge(bound, 10)
            dve.tensor_scalar(shift3[:, 0, :], norms[0], line[:, 0:1], line[:, 1:2], ALU.mult, ALU.add).then_inc(bound, 1)
            dve.tensor_scalar(beyond[:, 1:2], beyond[:, 1:2], -1.0, 1.0, ALU.mult, ALU.add).then_inc(bound, 1)
            dve.wait_ge(bound, 11)
            dve.wait_ge(beyond_mm, 1)
            dve.tensor_scalar(flag[:], ps[0:1, 0, 0:1], -2.0, None, ALU.mult).then_inc(flag_ready, 1)
            dve.wait_ge(flag_ready, 1)
            beyond_safe = dve.value_load(flag[0:1, 0:1], min_val=0, max_val=H)
            with dve.If(beyond_safe > 0):
                dve.memset(top[:, GH * T:P], 0.0).then_inc(max_read, 2)
                dve.sem_inc(top_ready, 1)
                with dve.Fori(0, NG) as gg:
                    for m in range(GH * T):
                        t = m % T
                        dve.wait_ge(max_mm, gg * (GH * T) + m + 1)
                        flat = ps[:, 4 * (m % 2):4 * (m % 2) + 4, :].rearrange("p b n -> p (b n)")
                        dve.tensor_reduce(top[:, m:m + 1], flat[:, 0:P * (t + 1)], AX, ALU.max).then_inc(max_read, 1)
                    dve.wait_ge(top_mm, gg + 2)
                    dve.wait_ge(top_out, gg * 16 + 16)
                    dve.tensor_scalar(topT[:], ps[0:GH * T, 0, 0:P], -1.0, None, ALU.mult).then_inc(top_ready, 1)
                dve.wait_ge(shift_in, 16)
                dve.tensor_copy(shift3[:, 0, :], shift).then_inc(true_shift, 1)
                dve.wait_ge(true_shift, 1)
                dve.tensor_tensor(shift_rest, shift, shift3[:, 0, :], ALU.subtract).then_inc(true_shift, 1)
                dve.wait_ge(true_shift, 2)
                dve.tensor_copy(shift3[:, 1, :], shift_rest).then_inc(true_shift, 1)
                dve.wait_ge(true_shift, 3)
                dve.tensor_tensor(shift3[:, 2, :], shift_rest, shift3[:, 1, :], ALU.subtract).then_inc(true_shift, 1)
                dve.wait_ge(true_shift, 4)
            dve.sem_inc(shift_ready, 1)

            dve.sem_inc(o_read, OB)
            with dve.Fori(0, NG // SETS) as i:
                for s in range(SETS):
                    for c in range(G):
                        no = i * (SETS * G) + (s * G + c)
                        b = c % OB
                        dve.wait_ge(pv_done, i * NB + (PB + s * (NB // SETS) + CHUNK_END[c] + 1))
                        dve.tensor_copy(o_sb[:, b, :], ps[:, 6 + b, :]).then_inc(o_copied, 1)
                        dve.wait_ge(o_turned, no + 1)
                        turned_o = ps[:, 6 + b, :].rearrange("p (t h v) -> p t h v", h=GH, v=VC)
                        dve.reciprocal(den[:, b, :, :], turned_o[:, :, :, HD]).then_inc(den_ready, 1)
                        dve.wait_ge(den_ready, no + 1)
                        dst = attn_tm[:, GT * c:GT * (c + 1), bass.ds(i * (SETS * GH * HD) + s * GH * HD, GH * HD)]
                        dve.tensor_tensor(dst.rearrange("p t (h d) -> p t h d", d=HD), turned_o[:, :, :, 0:HD],
                                          den[:, b, :, :].unsqueeze(3).to_broadcast([P, GT, GH, HD]),
                                          ALU.mult).then_inc(o_read, 1)
            feed_forward(1)

        @block.tensor
        def _(pe):
            def turn(kind, g, src):
                for k in range(GT):
                    ins = pe.transpose(ps[:, CHAIN + g % 2, P * k:P * (k + 1)], src[:, GT * g + k, :], ident[:])
                ins.then_inc(turned[kind], 1)

            def by_tile(bank, g, lhs, rhs, done):
                for k in range(GT):
                    n = P * (GT * g + k)
                    ins = pe.matmul(ps[:, bank, D * k:D * (k + 1)], lhs[:, n:n + P], rhs, start=True, stop=True)
                ins.then_inc(done, 1)

            misc_read = {"L": logit_sub, "R": kept, "K": coefT_ready}
            misc_steps = [(step, G * n + g) for n in range(2) for step, g in steps(n, "pe") if step in misc_read]

            def misc_free(step, q):
                at = misc_steps.index((step, q))
                if at:
                    last, of = misc_steps[at - 1]
                    pe.wait_ge(misc_read[last], of + 1)

            def feed_forward(n):
                for step, g in steps(n, "pe"):
                    q, bank = G * n + g, CHAIN + g % 2
                    if step in misc_read:
                        misc_free(step, q)
                    if step == "W":
                        pe.wait_ge(mha_in, 16 * MHA)
                        pe.matmul(ps[:, BIAS, 0:D], wv, woT, start=True, stop=True).then_inc(prep_mm, 1)
                        pe.wait_ge(prep_dve, 1)
                        pe.matmul(ps[:, BIAS, D:2 * D], bv_rep, woT, start=True, stop=True).then_inc(prep_mm, 1)
                        pe.wait_ge(prep_dve, 3)
                        pe.matmul(ps[:, BIAS, 2 * D:3 * D], centre[:], w_mha[:], start=True, stop=True).then_inc(prep_mm, 1)
                    elif step == "U":
                        if g >= 2:
                            pe.wait_ge(copied[OUT], g - 1)
                        for k in range(GT):
                            ins = pe.transpose(ps[:, g % 2, P * k:P * (k + 1)], attn_tm[:, GT * g + k, :], ident[:])
                        ins.then_inc(turned[OUT], 1)
                    elif step == "O":
                        pe.wait_ge(copied[OUT], g + 1)
                        if g >= 2:
                            pe.wait_ge(x_new, G + g - 1)
                        by_tile(2 + g % 2, g, oT, wqo[:, 1, :], out_mm)
                    elif step == "A":
                        if g >= 2:
                            pe.wait_ge(copied[Y1], q - 1)
                        pe.wait_ge(x_new if n else x_in[g], G + g + 1 if n else 16)
                        if n == 0:
                            pe.wait_ge(mha_in, 16 * MHA)
                        turn(ROWS, g, x_tm)
                    elif step == "P":
                        if n == 0:
                            pe.wait_ge(prep_dve, 4)
                        pe.wait_ge(copied[ROWS], q + 1)
                        by_tile(bank, g, xT, w_mha[:], mha_mm)
                    elif step == "C":
                        pe.wait_ge(normed[LN1], q + 1)
                        turn(Y1, g, y)
                    elif step == "L":
                        pe.wait_ge(copied[Y1], q + 1)
                        if n == 0:
                            pe.wait_ge(route_in, 16 * ROUTE)
                        for t in range(GT * g, GT * (g + 1)):
                            ins = pe.matmul(ps[:, MISC, E * t:E * (t + 1)], y1T[:, P * t:P * (t + 1)], wg[:],
                                            start=True, stop=True)
                        ins.then_inc(logit_mm, 1)
                    elif step == "R":
                        pe.wait_ge(pick_ready, 2 * q + 1)
                        first, end = GT * g, GT * (g + 1)
                        pe.matmul(ps[:, MISC, P + E * first:P + E * end], tri_bf[:, 0, :], pick_bf[:, E * first:E * end],
                                  start=True, stop=False)
                        for back in range(1, end):
                            at = max(first, back)
                            ins = pe.matmul(ps[:, MISC, P + E * at:P + E * end], tri_bf[:, 1, :],
                                            pick_bf[:, E * (at - back):E * (end - back)], start=False, stop=(back == end - 1))
                        ins.then_inc(place_mm, 1)
                    elif step == "D":
                        e = g
                        pe.wait_ge(w_in[e], 32)
                        for c in range(FC):
                            ins = pe.matmul(ps[:, e // 4, D * (e % 4):D * (e % 4 + 1)], w1T[:, e, c, :], w2[:, e, c, :],
                                            start=(c == 0), stop=(c == FC - 1))
                        if e % 4 == 3:
                            ins.then_inc(prep_mm, 1)
                        if e == 0:
                            pe.wait_ge(fold_in, 16 * FOLD)
                        for c in range(FC):
                            ins = pe.matmul(ps[:, 2, e:e + 1], w2[:, e, c, :], b1_t[:, c, e:e + 1],
                                            start=(c == 0), stop=(c == FC - 1))
                        if e == E - 1:
                            ins.then_inc(prep_mm, 1)
                    elif step == "H":
                        pe.wait_ge(prep_dve, 5)
                        pe.transpose(ps[0:TE, 2, P:2 * P], b12_cols.rearrange("p t e -> p (t e)"), ident[:]).then_inc(prep_mm, 1)
                        pe.wait_ge(att_in, 16 * 5)
                        for k in range(2):
                            ins = pe.matmul(ps[:, 3, D * k:D * (k + 1)], wdu[:, 0, :], wdu[:, 1 + k, :], start=True, stop=True)
                        ins.then_inc(prep_mm, 1)
                    elif step == "K":
                        pe.wait_ge(coef_ready, q + 1)
                        pe.transpose(ps[0:TE, MISC, P * (2 + g % 2):P * (3 + g % 2)],
                                     coef[:, group(g), :].rearrange("p t e -> p (t e)"), ident[:]).then_inc(coef_mm, 1)
                    elif step == "B":
                        if n == 0:
                            pe.wait_ge(prep_dve, 6)
                        pe.wait_ge(coefT_ready, q + 1)
                        if q >= 1:
                            pe.wait_ge(bias_read, q)
                        pe.matmul(ps[:, BIAS, :], coefT[:, g, :], b12_big[:].rearrange("p t d -> p (t d)"),
                                  start=True, stop=False)
                        for k in range(GT):
                            n0 = P * (GT * g + k)
                            ins = pe.matmul(ps[:, BIAS, D * k:D * (k + 1)], y1T[:, n0:n0 + P], ident[:],
                                            start=False, stop=(k == GT - 1))
                        ins.then_inc(bias_mm, 1)
                    elif step == "E":
                        t, k = g, T * n + g
                        if t == 0 and n == 0:
                            pe.wait_ge(prep_act, 2)
                            pe.wait_ge(prep_dve, 7)
                        if t == 0 and n == 1:
                            pe.wait_ge(x_new, 2 * G)
                        if t >= 2:
                            pe.wait_ge(high_ready, k - 1)
                        pe.matmul(ps[:, t % 2, :], y1T[:, P * t:P * (t + 1)], w12[:, 512:1024],
                                  start=True, stop=True).then_inc(high_mm, 1)
                        if t >= 2:
                            pe.wait_ge(pair_ready, k - 1)
                        pe.matmul(ps[:, 2 + t % 2, :], y1T[:, P * t:P * (t + 1)], w12[:, 0:512],
                                  start=True, stop=True).then_inc(low_mm, 1)
                    elif step == "T":
                        if g >= 2:
                            pe.wait_ge(copied[ATTN], g - 1)
                        pe.wait_ge(normed[ATTN], g + 1)
                        turn(ATTN, g, xn)

            feed_forward(0)

            pe.wait_ge(prep_dve, 11)
            for w in range(2 * G):
                g, side = w // 2, w % 2
                pe.wait_ge(copied[ATTN], g + 1 if g == 0 else G)
                if g >= 2:
                    pe.wait_ge(rope_part, 2 * (w - 4) + 2)
                for k, lhs in enumerate(((wqo[:, 0, :], wsw[:, 0, :]), (wkv[:, 0, :], wsw[:, 1, :]))[side]):
                    ins = pe.matmul(ps[:, 4 * (g % 2) + 2 * side + k, :], lhs, xT[:, cols(g)], start=True, stop=True)
                ins.then_inc(proj_mm, 1)
            pe.wait_ge(squared, 2 * G)
            pe.wait_ge(rope_part, 2 * 2 * G)
            for side in range(2):
                for g in range(G):
                    ins = pe.matmul(ps[0:H, 4 * (1 - side) + g, :], head_of[:], square[:, 2 * g + side, :],
                                    start=True, stop=True)
                ins.then_inc(norm_mm, 1)
            pe.wait_ge(bound, 2)
            for g in range(G):
                by_tile(g, g, xT, wkv[:, 1, :], v_mm)
            pe.wait_ge(v_ready, G)
            pe.wait_ge(bound, 12)
            pe.matmul(ps[0:1, 0, 0:1], beyond[:, 1:2], neg_half[0:H, 0:1], start=True, stop=True).then_inc(beyond_mm, 1)
            pe.wait_ge(flag_ready, 1)
            beyond_safe = pe.value_load(flag[0:1, 0:1], min_val=0, max_val=H)
            with pe.If(beyond_safe > 0):
                pe.sem_inc(top_mm, 1)
                with pe.Fori(0, NG) as gg:
                    pe.wait_ge(max_in, gg * (16 * PACK_DMAS) + 16 * PACK_DMAS)
                    pe.wait_ge(top_ready, gg + 1)
                    for m in range(GH * T):
                        h, t = m // T, m % T
                        pe.wait_ge(max_read, gg * (GH * T) + m + 1)
                        for n in range(0, P * (t + 1), 512):
                            w = min(512, P * (t + 1) - n)
                            ins = pe.matmul(ps[:, 4 * (m % 2) + n // 512, 0:w], packed[:, 0, 0, h, P * t:P * (t + 1)],
                                            packed[:, 0, 1, h, n:n + w], start=True, stop=True)
                        ins.then_inc(max_mm, 1)
                    pe.wait_ge(max_read, gg * (GH * T) + GH * T + 2)
                    pe.transpose(ps[:, 0, 0:P], top[:], ident[:]).then_inc(top_mm, 1)
                pe.wait_ge(top_ready, 1 + NG)

            pe.sem_inc(pv_done, PB)
            with pe.Fori(0, NG // SETS) as i:
                def scores(n):
                    s, first = n // (NE // SETS), 2 * (n % (NE // SETS))
                    if first == 0:
                        pe.wait_ge(packed_in[s], i * (16 * (PACK_DMAS + 1)) + 16 * (PACK_DMAS + 1))
                    pe.wait_ge(exp_done, i * NE + (EB + previous_exp(n) + 1))
                    for b in range(2):
                        for h, j, q, w, col in BANKS[first + b]:
                            ins = pe.matmul(ps[:, 2 * (n % EB) + b, col:col + w], packed[:, s, 1, h, P * j:P * (j + 1)],
                                            packed[:, s, 0, h, q:q + w], start=True, stop=True)
                    ins.then_inc(score_mm, 1)

                def values(m):
                    s, first = m // (NB // SETS), 4 * (m % (NB // SETS))
                    if first == 0:
                        pe.wait_ge(v_staged, i * SETS + s + 2)
                    pe.wait_ge(exp_done, i * NE + (EB + 2 * m + 2))
                    for b in range(4):
                        for h, j, q, w, col in BANKS[first + b]:
                            c = chunk_of((h, j, q, w, col))
                            if j == 0 and h == 0:
                                pe.wait_ge(o_read, i * (SETS * G) + (s * G + c + 1))
                            last = j == GT * c + 2
                            ins = pe.matmul(ps[32 * h:32 * h + VC, 6 + c % OB, q - GW * c:q - GW * c + w],
                                            v_st[:, s, j, h, :], pexp[:, 2 * (m % PB) + b // 2, 512 * (b % 2) + col:512 * (b % 2) + col + w],
                                            start=(j == 0), stop=last, tile_position=(0, 32 * h), skip_group_check=True)
                    ins.then_inc(pv_done, 1)

                def turn_output(k):
                    pe.wait_ge(o_copied, i * (SETS * G) + k + 1)
                    for j in range(GT):
                        ins = pe.transpose(ps[:, 6 + k % G % OB, P * j:P * (j + 1)], o_sb[:, k % OB, P * j:P * (j + 1)], ident[:])
                    ins.then_inc(o_turned, 1)

                turning = {min(s * (NB // SETS) + CHUNK_END[c] + LAG, NB - 1): s * G + c for s in range(SETS) for c in range(G)}
                scores(0)
                scores(1)
                for m in range(NB):
                    for n in (2 * m + 2, 2 * m + 3):
                        if n < NE:
                            scores(n)
                    values(m)
                    if m in turning:
                        turn_output(turning[m])
            pe.wait_ge(o_read, OB + NG * G)
            feed_forward(1)


PREP_MM, PREP_DVE = 8, 7
CHUNK_END = [max(n for n, bank in enumerate(BANKS) if chunk_of(bank[0]) == c) // 4 for c in range(G)]


def bf16_bits(x):
    return (x.astype(np.float32).view(np.uint32) >> 16).astype(np.uint16)


def constants():
    inv = 1.0 / 10000.0 ** (np.arange(0, HD, 2, dtype=np.float32) / HD)
    ang = np.outer(np.arange(S, dtype=np.float32), inv)
    rope = np.stack([np.cos(ang), np.sin(ang)]).astype(np.float32)
    rope = np.tile(np.repeat(rope.transpose(0, 2, 1), 2, axis=1), (1, H, 1))
    te = np.arange(P)
    page = np.arange(S) // PAGE
    q_side = np.zeros((P - SHIFT_ROW, S))
    k_side = np.zeros((P - SHIFT_ROW, S))
    k_side[0:3] = 1
    rel = MASK_ROW - SHIFT_ROW
    q_side[rel:] = np.arange(PAGES)[:, None] > page[None, :]
    k_side[rel:] = np.where(np.arange(PAGES)[:, None] == page[None, :], MASKED, 0.0)
    return {
        "ident": np.eye(P, dtype=np.float32),
        "centre": (np.eye(P) - 1.0 / D).astype(np.float32),
        "tri": bf16_bits(np.stack([np.triu(np.ones((P, P))), np.ones((P, P))], axis=1)),
        "tile_is": (te[:TE, None] // E == np.arange(GT)[None, :]).astype(np.float32),
        "rank": np.tile(E - np.arange(E, dtype=np.float32), T),
        "head_of": bf16_bits(te[:, None] // HD == np.arange(H)[None, :]),
        "rope": rope,
        "template": bf16_bits(np.stack([q_side, k_side])),
    }


def kernel(**inputs):
    import concourse.bacc as _bacc
    from concourse.bass_utils import run_bass_kernel_spmd as _run

    v = {k: np.asarray(x) for k, x in inputs.items()}
    arrays = {
        "x": v["L0_attn_x"].reshape(S, D),
        "wv": v["L0_ffn_in_proj_w"][2 * D:3 * D], "bv": v["L0_ffn_in_proj_b"][2 * D:3 * D].reshape(D, 1),
        "woT": v["L0_ffn_out_proj_w"].T, "ob": v["L0_ffn_out_proj_b"],
        "g1c": np.stack([v["L0_ffn_ln1_g"], v["L0_ffn_ln1_b"]], axis=1),
        "lnb": np.stack([v["L0_ffn_ln2_g"], v["L0_ffn_ln2_b"]]),
        "wg": v["L0_ffn_wg"], "w1T": v["L0_ffn_w1"].transpose(0, 2, 1), "w2": v["L0_ffn_w2"],
        "b1_t": v["L0_ffn_b1"].reshape(E, P, FC).transpose(1, 2, 0), "b2_t": v["L0_ffn_b2"].T,
        "wq": v["L0_attn_wq"], "wo": v["L0_attn_wo"], "w_downT": v["L0_attn_w_down"].T,
        "wk_up": v["L0_attn_wk_up"], "wv_up": v["L0_attn_wv_up"],
    }
    arrays.update(constants())
    arrays = {k: np.ascontiguousarray(x) for k, x in arrays.items()}
    nc = _bacc.Bacc("TRN2", target_bir_lowering=False, num_devices=1)
    a = {k: nc.dram_tensor(f"in_{k}", x.shape, mybir.dt.from_np(x.dtype), kind="ExternalInput").ap()
         for k, x in arrays.items()}
    out = nc.dram_tensor("out_rows", (S, D), F32, kind="ExternalOutput").ap()
    build(nc, a, out)
    r = _run(nc, [{f"in_{k}": x for k, x in arrays.items()}], core_ids=[0])
    return r.results[0]["out_rows"].reshape(1, S, D)
```
